# Optimizing a Trainium2 kernel written in Bass

```python
import numpy as np
import jax
import jax.numpy as jnp

def _softmax(x, axis=-1):
    return jax.nn.softmax(x, axis=axis)

def _gelu(x):
    return jax.nn.gelu(x, approximate=True)

def _silu(x):
    return jax.nn.silu(x)

def _sigmoid(x):
    return jax.nn.sigmoid(x)

def _layernorm(x, axis=-1, eps=1e-05):
    m = jnp.mean(x, axis=axis, keepdims=True)
    v = jnp.var(x, axis=axis, keepdims=True)
    return (x - m) / jnp.sqrt(v + eps)

def _scatter_add(tgt, idx, src, axis=0):
    return tgt.at[idx].add(src)

def _segment_sum(src, seg, n):
    return jax.ops.segment_sum(src, seg, n)
kernel_name = 'mk_vit_tower_d1_tok_img768_r4_b7b4ca'

def setup_inputs(seed: int=0):
    np.random.seed(seed)
    _w = jnp.asarray

    def _rec_inputs():
        import jax
        import jax.numpy as jnp
        _rk = jax.random.key(seed)
        x = 7.57192e-06 + 1.00007 * jax.random.normal(jax.random.fold_in(_rk, 1), (16, 3, 96, 96), jnp.float32)
        return x
    x = _rec_inputs()

    def _L0_tok_setup():
        import jax, jax.numpy as jnp
        import numpy as np
        PH, PW = (16, 16)
        key = jax.random.key(seed)
        k1, k2, k3 = jax.random.split(key, 3)
        B, C, H, Wd = (64, 3, 224, 224)
        embed_dim = 192
        input_dim = C * PH * PW
        images = jax.random.normal(k1, (B, C, H, Wd), dtype=jnp.float32)
        W = jax.random.normal(k2, (embed_dim, input_dim), dtype=jnp.float32) * 0.02
        b = jax.random.normal(k3, (embed_dim,), dtype=jnp.float32) * 0.02
        return {'images': images, 'W': W, 'b': b}
    _L0_tok_all = _L0_tok_setup()
    _L0_tok_in = {k: v for k, v in _L0_tok_all.items() if k in ('W', 'b')}
    del _L0_tok_all

    def _L0_attn_setup():
        import jax, jax.numpy as jnp
        import numpy as np

        def depthwise_conv1d(x, w, pad):
            return jax.lax.conv_general_dilated(x, w, window_strides=(1,), padding=[(pad, pad)], dimension_numbers=('NCH', 'OIH', 'NCH'), feature_group_count=x.shape[1])
        key = jax.random.key(seed)
        ks = jax.random.split(key, 6)
        B, L, D, F = (2, 512, 192, 64)
        return {'x': jax.random.normal(ks[0], (B, L, D), jnp.float32), 'w_in': jax.random.normal(ks[1], (D, 4 * D), jnp.float32) * D ** (-0.5), 'b_in': jnp.zeros((4 * D,), jnp.float32), 'w_filt': jax.random.normal(ks[2], (F, D), jnp.float32) * F ** (-0.5), 'b_filt': jnp.zeros((D,), jnp.float32), 'w_short': jax.random.normal(ks[3], (D, 1, 3), jnp.float32) * 0.5, 'b_short': jnp.zeros((D,), jnp.float32), 'w_out': jax.random.normal(ks[4], (D, D), jnp.float32) * D ** (-0.5), 'b_out': jnp.zeros((D,), jnp.float32)}
    _L0_attn_all = _L0_attn_setup()
    _L0_attn_in = {k: v for k, v in _L0_attn_all.items() if k in ('w_in', 'b_in', 'w_filt', 'b_filt', 'w_short', 'b_short', 'w_out', 'b_out')}
    del _L0_attn_all

    def _L0_ffn_setup():
        import jax, jax.numpy as jnp
        import numpy as np
        EMB = 192
        HID = 288
        NUM_EXPERTS = 8
        TOP_K = 2
        key = jax.random.key(seed)
        ks = jax.random.split(key, 8)
        s = 0.02
        x = jax.random.normal(ks[0], (4, 256, EMB), dtype=jnp.float32)
        router_w = jax.random.normal(ks[1], (EMB, NUM_EXPERTS), dtype=jnp.float32) * s
        router_b = jnp.zeros((NUM_EXPERTS,), dtype=jnp.float32)
        w1 = jax.random.normal(ks[2], (NUM_EXPERTS, EMB, HID), dtype=jnp.float32) * s
        b1 = jnp.zeros((NUM_EXPERTS, HID), dtype=jnp.float32)
        w2 = jax.random.normal(ks[3], (NUM_EXPERTS, HID, EMB), dtype=jnp.float32) * s
        b2 = jnp.zeros((NUM_EXPERTS, EMB), dtype=jnp.float32)
        return {'x': x, 'router_w': router_w, 'router_b': router_b, 'w1': w1, 'b1': b1, 'w2': w2, 'b2': b2}
    _L0_ffn_all = _L0_ffn_setup()
    _L0_ffn_in = {k: v for k, v in _L0_ffn_all.items() if k in ('router_w', 'router_b', 'w1', 'b1', 'w2', 'b2')}
    del _L0_ffn_all
    return {'x': x, 'L0_tok_W': _L0_tok_in['W'], 'L0_tok_b': _L0_tok_in['b'], 'L0_attn_w_in': _L0_attn_in['w_in'], 'L0_attn_b_in': _L0_attn_in['b_in'], 'L0_attn_w_filt': _L0_attn_in['w_filt'], 'L0_attn_b_filt': _L0_attn_in['b_filt'], 'L0_attn_w_short': _L0_attn_in['w_short'], 'L0_attn_b_short': _L0_attn_in['b_short'], 'L0_attn_w_out': _L0_attn_in['w_out'], 'L0_attn_b_out': _L0_attn_in['b_out'], 'L0_ffn_router_w': _L0_ffn_in['router_w'], 'L0_ffn_router_b': _L0_ffn_in['router_b'], 'L0_ffn_w1': _L0_ffn_in['w1'], 'L0_ffn_b1': _L0_ffn_in['b1'], 'L0_ffn_w2': _L0_ffn_in['w2'], 'L0_ffn_b2': _L0_ffn_in['b2']}

def reference(x, L0_tok_W, L0_tok_b, L0_attn_w_in, L0_attn_b_in, L0_attn_w_filt, L0_attn_b_filt, L0_attn_w_short, L0_attn_b_short, L0_attn_w_out, L0_attn_b_out, L0_ffn_router_w, L0_ffn_router_b, L0_ffn_w1, L0_ffn_b1, L0_ffn_w2, L0_ffn_b2):
    import jax
    import jax.numpy as jnp

    def _L0_tok_ref(images, W, b):
        import jax, jax.numpy as jnp
        import numpy as np
        PH, PW = (16, 16)
        B, C, H, Wd = images.shape
        Hn, Wn = (H // PH, Wd // PW)
        x = images.reshape(B, C, Hn, PH, Wn, PW)
        x = x.transpose(0, 2, 4, 1, 3, 5)
        x = x.reshape(B, Hn * Wn, C * PH * PW)
        return jnp.einsum('bnd,ed->bne', x, W) + b

    def _L0_attn_ref(x, w_in, b_in, w_filt, b_filt, w_short, b_short, w_out, b_out):
        import jax, jax.numpy as jnp
        import numpy as np

        def depthwise_conv1d(x, w, pad):
            return jax.lax.conv_general_dilated(x, w, window_strides=(1,), padding=[(pad, pad)], dimension_numbers=('NCH', 'OIH', 'NCH'), feature_group_count=x.shape[1])
        B, L, D = x.shape
        F = w_filt.shape[0]
        x_short = depthwise_conv1d(x.transpose(0, 2, 1), w_short, 1).transpose(0, 2, 1) + b_short
        proj = x @ w_in + b_in
        x_proj, z_proj, v1, v2 = jnp.split(proj, 4, axis=-1)
        z = jax.nn.silu(z_proj)
        t = jnp.arange(L, dtype=jnp.float32)[:, None]
        f = jnp.arange(F, dtype=jnp.float32)[None, :]
        pos_basis = jnp.sin(t * f / F)
        filt = (pos_basis @ w_filt + b_filt).T
        conv = depthwise_conv1d(x_proj.transpose(0, 2, 1), filt[:, None, :], L // 2)[:, :, :L]
        y = conv.transpose(0, 2, 1) * v1 * v2 * z
        return (y + x_short) @ w_out + b_out

    def _L0_ffn_ref(x, router_w, router_b, w1, b1, w2, b2):
        import jax, jax.numpy as jnp
        import numpy as np
        EMB = 192
        HID = 288
        NUM_EXPERTS = 8
        TOP_K = 2
        B, N, E = x.shape
        T = B * N
        logits = jnp.einsum('bne,ef->bnf', x, router_w) + router_b
        probs = jax.nn.softmax(logits, axis=-1)
        topk_probs, topk_idx = jax.lax.top_k(probs, TOP_K)
        flat_x = x.reshape(T, E)
        flat_idx = topk_idx.reshape(T, TOP_K)
        flat_w = topk_probs.reshape(T, TOP_K)
        gates = jnp.zeros((T, NUM_EXPERTS), dtype=x.dtype)
        gates = gates.at[jnp.arange(T)[:, None], flat_idx].add(flat_w)
        out = jnp.zeros((T, E), dtype=x.dtype)
        for e in range(NUM_EXPERTS):
            h = jax.nn.gelu(flat_x @ w1[e] + b1[e], approximate=False)
            y = h @ w2[e] + b2[e]
            out = out + y * gates[:, e:e + 1]
        return out.reshape(B, N, E)
    h = _L0_tok_ref(x, L0_tok_W, L0_tok_b)
    h = h + _L0_attn_ref(_layernorm(h, axis=-1), L0_attn_w_in, L0_attn_b_in, L0_attn_w_filt, L0_attn_b_filt, L0_attn_w_short, L0_attn_b_short, L0_attn_w_out, L0_attn_b_out)
    h = h + _L0_ffn_ref(_layernorm(h, axis=-1), L0_ffn_router_w, L0_ffn_router_b, L0_ffn_w1, L0_ffn_b1, L0_ffn_w2, L0_ffn_b2)
    return h

_drawn_inputs = setup_inputs


def setup_inputs(seed=0):
    import zlib

    import numpy as np

    out = dict(_drawn_inputs(seed))
    spreads = {'L0_attn_b_in': (0.0, 0.1),
     'L0_attn_b_filt': (0.0, 0.1),
     'L0_attn_b_short': (0.0, 0.306),
     'L0_attn_b_out': (0.0, 0.3),
     'L0_ffn_router_b': (0.0, 0.8),
     'L0_ffn_b1': (0.0, 0.8),
     'L0_ffn_b2': (0.0, 0.8)}
    factors = {'L0_ffn_router_w': 8.0, 'L0_ffn_w1': 8.0, 'L0_ffn_w2': 8.0}
    for name, (base, spread) in spreads.items():
        noise = np.random.default_rng([zlib.crc32(name.encode()), seed]).standard_normal(out[name].shape)
        drawn = base * np.exp(spread * noise) if base else spread * noise
        out[name] = jnp.asarray(drawn.astype(out[name].dtype))
    for name, factor in factors.items():
        out[name] = (out[name] * factor).astype(out[name].dtype)
    return out
```

```python
import concourse.bass as bass
from concourse import mybir
from contextlib import ExitStack

D = 192
DA, DB = 128, 64
IMAGES, SEQ = 16, 36
TOK = IMAGES * SEQ
TT = [(s, min(128, TOK - s)) for s in range(0, TOK, 128)]
NT = len(TT)
PIX = 768
KP = PIX // 128
PAIRS = IMAGES // 2
PTOK = 2 * SEQ
POINTS = 54
PF = 2 * POINTS
HALF = TOK // 2
HIM = IMAGES // 2
TAPS = 64
E = 8
HID = 288
HC = E * HID // 128
GATE_COL = [(192, 128), (320, 128), (448, 128), (576, 128), (704, 64)]
P_BZA, P_BZB, P_BV1A, P_BV2A, P_BV2B, P_WSA, P_WSB, P_BSA, P_BSB, P_B1 = 0, 1, 2, 3, 4, 5, 8, 11, 12, 13
NPAR = P_B1 + HC
CHUNKS = [(0, 1), (2, 3, 4)]
EPS = 1e-5
PIECES = 6
W1P = HC * 128 // PIECES
W2P = HC // PIECES
RING = 5
G_LAG, DOWN_LAG = 2, 4


def build(nc, xt, tokw, tokb, win_a, win_b, binx, par, wo_a, wo_b, bout, waug, rw_a, rw_b, rb,
          w1, w2, b2, c_basis, c_fwd, c_inv, c_sel, c_ident, c_iota, out):
    f32, f32r, u32 = mybir.dt.float32, mybir.dt.float32r, mybir.dt.uint32
    ALU, ACT, AX = mybir.AluOpType, mybir.ActivationFunctionType, mybir.AxisListType
    ctx = ExitStack()
    with ctx:
        def sb(name, shape, dt=f32):
            return ctx.enter_context(nc.sbuf_tensor(name, shape, dt))

        def sem(name):
            return ctx.enter_context(nc.semaphore(name))

        x_s = sb("x_s", [128, KP * TOK])
        tokw_s = sb("tokw_s", [128, KP, D])
        tokb_s = sb("tokb_s", [128, D])
        win_s = sb("win_s", [128, 2, 4 * D])
        win_h = sb("win_h", [128, 2, 4 * D], f32r)
        win_l = sb("win_l", [128, 2, 4 * D], f32r)
        binx_s = sb("binx_s", [PTOK, D])
        par_s = sb("par_s", [128, NPAR])
        woa_s = sb("woa_s", [DA, D])
        wob_s = sb("wob_s", [DB, D])
        bout_s = sb("bout_s", [128, D])
        waug_s = sb("waug_s", [TAPS + 1, D])
        rw_s = sb("rw_s", [128, 2, E])
        rw_h = sb("rw_h", [128, 2, E], f32r)
        rw_l = sb("rw_l", [128, 2, E], f32r)
        rb_s = sb("rb_s", [128, E])
        stage = sb("stage", [128, PIECES, 2 * W1P])
        w1_h = sb("w1_h", [128, 2, HC * 128], f32r)
        w1_l = sb("w1_l", [128, 2, HC * 128], f32r)
        w2_h = sb("w2_h", [128, HC, D], f32r)
        w2_l = sb("w2_l", [128, HC, D], f32r)
        b2_s = sb("b2_s", [2 * E, D])
        b2_h = sb("b2_h", [2 * E, D], f32r)
        b2_l = sb("b2_l", [2 * E, D], f32r)
        basis_s = sb("basis_s", [TAPS + 1, 2, PF])
        fwd_s = sb("fwd_s", [PTOK, PF])
        inv_s = sb("inv_s", [PF, 2, PTOK])
        sel_r = sb("sel_r", [2 * E, HC * 128], f32r)
        ident_s = sb("ident_s", [128, 128])
        iota_s = sb("iota_s", [128, E])
        eps_s = sb("eps_s", [128, 1])
        h_s = sb("h_s", [128, NT, D])
        hb_s = sb("hb_s", [128, NT, D])
        h2_s = sb("h2_s", [128, NT, D])
        o_s = h_s
        st = [sb(f"st{n}", [128, NT, 6]) for n in range(2)]
        mv = [sb(f"mv{n}", [128, NT, 2]) for n in range(2)]
        sd = [sb(f"sd{n}", [128, NT]) for n in range(2)]
        rs = [sb(f"rs{n}", [128, NT]) for n in range(2)]
        xn = [sb("xn", [128, NT, 2 * DA])] * 2
        xt32 = [sb("xt32", [128, 2, TOK])] * 2
        xth = [sb("xth", [128, 2, TOK], f32r)] * 2
        xtl = [sb("xtl", [128, TOK], f32r)] * 2
        spec_s = sb("spec_s", [PF, 2, D])
        xp_s = win_s[:PTOK, :, :].rearrange("p a n -> p (a n)").rearrange("p (g d) -> p g d", d=D)
        p_s = [x_s[:PF, n * PAIRS * D:(n + 1) * PAIRS * D].rearrange("p (g d) -> p g d", d=D) for n in range(2)]
        zs_a = sb("zs_a", [DA, 2, HALF])
        zs_b = sb("zs_b", [128, 2, HALF])
        u_a = g_a = zs_a
        u_b = sb("u_b", [DB, 2, HALF])
        g_b = u_b
        xs_a = sb("xs_a", [DA, TOK])
        xs_b = sb("xs_b", [DB, TOK])
        yt_a = y_a = sb("y_a", [DA, TOK])
        yt_b = y_b = sb("y_b", [DB, TOK])
        lg = sb("lg", [128, NT, E])
        mx = sb("mx", [128, NT, E])
        ix = sb("ix", [128, NT, E], u32)
        ixf = sb("ixf", [128, NT, 2])
        dl = sb("dl", [128, NT, E])
        ex = sb("ex", [128, NT, E])
        m1 = sb("m1", [128, NT, E])
        m2 = sb("m2", [128, NT, E])
        mk = sb("mk", [128, NT, E])
        em = sb("em", [128, NT, E])
        se = sb("se", [128, NT])
        re = sb("re", [128, NT])
        gt = sb("gt", [128, NT, E])
        ghl = sb("ghl", [128, NT, 2 * E])
        gT = sb("gT", [2 * E, TOK], f32r)
        CW = max(sum(TT[t][1] for t in ts) for ts in CHUNKS)
        ge, gm = (x_s[:, n * RING * CW:(n + 1) * RING * CW].rearrange("p (r c) -> p r c", c=CW) for n in range(2))
        gmh = sb("gmh", [128, RING, CW], f32r)
        gml = sb("gml", [128, RING, CW], f32r)

        bank = [ctx.enter_context(nc.psum_tensor(f"bank{i}", [128, 512], f32)) for i in range(8)]

        ld_tokw, ld_sm, ld_win, ld_wo, ld_sel, ld_cst, stored = map(
            sem, ["ld_tokw", "ld_sm", "ld_win", "ld_wo", "ld_sel", "ld_cst", "stored"])
        ld_w1, ld_w2 = ([sem(f"ld_{n}_{q}") for q in range(PIECES)] for n in ("w1", "w2"))
        ld_x = [sem(f"ld_x{t}") for t in range(NT)]
        tok_done, spec_mm, tr_done, px_done, fwd_done, gate_mm, inv_done, wo_done = map(
            sem, ["tok_done", "spec_mm", "tr_done", "px_done", "fwd_done", "gate_mm", "inv_done", "wo_done"])
        tr2_done, rt_done, gtr_done, up_done, gb_done, down_done, acc_done = map(
            sem, ["tr2_done", "rt_done", "gtr_done", "up_done", "gb_done", "down_done", "acc_done"])
        win_hi, w1_hi, w2_hi, sm_hi, win_lo, w1_lo, w2_lo, sm_lo = map(
            sem, ["win_hi", "w1_hi", "w2_hi", "sm_hi", "win_lo", "w1_lo", "w2_lo", "sm_lo"])
        eps_set, lg_set, spec_ev, h_ready, hb_ready, h2_ready = map(
            sem, ["eps_set", "lg_set", "spec_ev", "h_ready", "hb_ready", "h2_ready"])
        stat, var_ready, sd_ready, rs_ready, xn_ready, xt_ready, hi_ready, split = (
            [sem(f"{n}{k}") for k in (1, 2)] for n in
            ("stat", "var_ready", "sd_ready", "rs_ready", "xn_ready", "xt_ready", "hi_ready", "split"))
        px_ev, spec_mul, silu_done, gate_done, xs_mid, xs_step, y_done, yt_done = map(
            sem, ["px_ev", "spec_mul", "silu_done", "gate_done", "xs_mid", "xs_step", "y_done", "yt_done"])
        lg_ev, mx_ready, dl_ready, ix_ready, best, exp_done, sum_ready, ghl_ready, gT_ready = map(
            sem, ["lg_ev", "mx_ready", "dl_ready", "ix_ready", "best", "exp_done", "sum_ready", "ghl_ready", "gT_ready"])
        gelu_done, gm_done, gmh_done, gml_done, fin_done = map(
            sem, ["gelu_done", "gm_done", "gmh_done", "gml_done", "fin_done"])

        NSM = 8
        NCST = 6
        steps = [(c, j) for c in range(len(CHUNKS)) for j in range(HC)]
        NS = len(steps)

        def chunk_cols(c):
            s = TT[CHUNKS[c][0]][0]
            return s, sum(TT[t][1] for t in CHUNKS[c])

        def piece1(q):
            return stage[:, q, :].rearrange("p (a n) -> p a n", a=2)

        def piece2(q):
            return stage[:, q, :W2P * D].rearrange("p (j d) -> p j d", d=D)

        def tile_of(token):
            return token // 128

        block = ctx.enter_context(nc.Block())

        @block.sync
        def _(sp):
            for t, (s, n) in enumerate(TT):
                sp.dma_start(x_s[:, KP * s:KP * (s + n)], xt[:, KP * s:KP * (s + n)]).then_inc(ld_x[t], 16)
                if t == 1:
                    sp.dma_start(win_s[:, 0, :], win_a).then_inc(ld_win, 16)
                    sp.dma_start(win_s[:, 1, :], win_b).then_inc(ld_win, 16)
            for q in range(PIECES):
                sp.dma_start(stage[:, q, :], w1[:, q, :]).then_inc(ld_w1[q], 16)
            for q in range(PIECES):
                sp.wait_ge(w1_lo, q + 1)
                sp.dma_start(stage[:, q, :W2P * D], w2[:, q, :]).then_inc(ld_w2[q], 16)
            for t, (s, n) in enumerate(TT):
                sp.wait_ge(fin_done, t + 1)
                sp.dma_start(out[s:s + n, :], o_s[:n, t, :]).then_inc(stored, 16)
            sp.wait_ge(stored, 16 * NT)

        @block.gpsimd
        def _(pool):
            nc.gpsimd.memset(eps_s[:, :], EPS).then_inc(eps_set, 1)
            nc.gpsimd.memset(lg[:, :, :], 0.0).then_inc(lg_set, 1)
            pool.dma_start(sel_r[:, :], c_sel).then_inc(ld_sel, 16)
            pool.wait_ge(sm_hi, 2)
            pool.wait_ge(ld_sm, 16 * NSM)
            nc.gpsimd.tensor_tensor(rw_l[:, :, :], rw_s[:, :, :], rw_h[:, :, :].bitcast(f32), ALU.subtract).then_inc(sm_lo, 1)
            nc.gpsimd.tensor_tensor(b2_l[:, :], b2_s[:, :], b2_h[:, :].bitcast(f32), ALU.subtract).then_inc(sm_lo, 1)
            for t, (s, n) in enumerate(TT):
                pool.wait_ge(h_ready, t + 1)
                nc.gpsimd.tensor_tensor(hb_s[:n, t, :], h_s[:n, t, :], bout_s[:n, :], ALU.add).then_inc(hb_ready, 1)
            for q in range(PIECES):
                pool.wait_ge(w1_hi, q + 1)
                c = slice(q * W1P, (q + 1) * W1P)
                nc.gpsimd.tensor_tensor(w1_l[:, :, c], piece1(q), w1_h[:, :, c].bitcast(f32), ALU.subtract).then_inc(w1_lo, 1)
            for q in range(PIECES):
                pool.wait_ge(w2_hi, q + 1)
                c = slice(q * W2P, (q + 1) * W2P)
                nc.gpsimd.tensor_tensor(w2_l[:, c, :], piece2(q), w2_h[:, c, :].bitcast(f32), ALU.subtract).then_inc(w2_lo, 1)

        @block.scalar
        def _(act):
            act.dma_start(tokw_s[:, :, :], tokw).then_inc(ld_tokw, 16)
            for dst, src in ((tokb_s, tokb), (binx_s, binx), (bout_s, bout), (rb_s, rb)):
                act.dma_start(dst[:, :], src.partition_broadcast(dst.shape[0])).then_inc(ld_sm, 16)
            act.dma_start(rw_s[:, 0, :], rw_a).then_inc(ld_sm, 16)
            act.dma_start(rw_s[:, 1, :], rw_b).then_inc(ld_sm, 16)
            act.dma_start(par_s[:, :], par).then_inc(ld_sm, 16)
            act.dma_start(b2_s[:, :], b2).then_inc(ld_sm, 16)
            act.dma_start(waug_s[:, :], waug).then_inc(ld_cst, 16)
            act.dma_start(basis_s[:, :, :], c_basis).then_inc(ld_cst, 16)
            act.dma_start(ident_s[:, :], c_ident).then_inc(ld_cst, 16)
            act.dma_start(fwd_s[:, :], c_fwd).then_inc(ld_cst, 16)
            act.dma_start(inv_s[:, :, :], c_inv).then_inc(ld_cst, 16)
            act.dma_start(iota_s[:, :], c_iota.partition_broadcast(128)).then_inc(ld_cst, 16)
            act.dma_start(woa_s[:, :], wo_a).then_inc(ld_wo, 16)
            act.dma_start(wob_s[:, :], wo_b).then_inc(ld_wo, 16)

            def cut_high(dst, src, done):
                nc.scalar.activation(dst, src, ACT.Copy).then_inc(done, 1)

            def deviation(n, t):
                rows = TT[t][1]
                act.wait_ge(var_ready[n], t + 1)
                nc.scalar.activation(sd[n][:rows, t:t + 1], mv[n][:rows, t, 1:2], ACT.Sqrt,
                                     bias=eps_s[:rows, :]).then_inc(sd_ready[n], 1)

            def evacuate(n, t, done, banks):
                s, rows = TT[t]
                act.wait_ge(done, t + 1)
                src = bank[banks + t % 2][:, 0:256].rearrange("p (a c) -> p a c", a=2)[:, :, :rows]
                nc.scalar.activation(xt32[n][:, :, s:s + rows], src, ACT.Copy).then_inc(xt_ready[n], 1)

            act.wait_ge(ld_win, 32)
            cut_high(win_h[:, 0, :], win_s[:, 0, :], win_hi)
            cut_high(win_h[:, 1, :], win_s[:, 1, :], win_hi)
            act.wait_ge(eps_set, 1)
            for t in range(NT):
                deviation(0, t)
                if t >= 2:
                    evacuate(0, t - 2, tr_done, 2)
            act.wait_ge(ld_sm, 16 * NSM)
            cut_high(rw_h[:, :, :], rw_s[:, :, :], sm_hi)
            cut_high(b2_h[:, :], b2_s[:, :], sm_hi)

            def short_mid(h):
                act.wait_ge(xt_ready[0], (3, NT)[h])
                c = slice(h * HALF, (h + 1) * HALF)
                nc.scalar.activation(xs_a[:, c], xt32[0][:, 0, c], ACT.Identity, bias=par_s[:, P_BSA:P_BSA + 1],
                                     scale=par_s[:, P_WSA + 1:P_WSA + 2]).then_inc(xs_mid, 1)
                nc.scalar.activation(xs_b[:, c], xt32[0][0:DB, 1, c], ACT.Identity, bias=par_s[0:DB, P_BSB:P_BSB + 1],
                                     scale=par_s[0:DB, P_WSB + 1:P_WSB + 2]).then_inc(xs_mid, 1)

            def silus(h):
                act.wait_ge(gate_mm, 5 * h + 1)
                nc.scalar.activation(zs_a[:, h, :], bank[6 + (5 * h) % 2][:, :HALF], ACT.Silu,
                                     bias=par_s[:, P_BZA:P_BZA + 1]).then_inc(silu_done, 1)
                act.wait_ge(gate_mm, 5 * h + 2)
                nc.scalar.activation(zs_b[64:128, h, :], bank[6 + (5 * h + 1) % 2][0:64, :HALF], ACT.Silu,
                                     bias=par_s[0:64, P_BZB:P_BZB + 1]).then_inc(silu_done, 1)

            short_mid(0)
            silus(0)
            evacuate(0, 3, tr_done, 2)
            evacuate(0, 4, tr_done, 2)
            short_mid(1)
            silus(1)
            for q in range(PIECES):
                act.wait_ge(ld_w1[q], 16)
                cut_high(w1_h[:, :, q * W1P:(q + 1) * W1P], piece1(q), w1_hi)
            for q in range(PIECES):
                act.wait_ge(ld_w2[q], 16)
                cut_high(w2_h[:, q * W2P:(q + 1) * W2P, :], piece2(q), w2_hi)
            for t in range(NT):
                deviation(1, t)
                if t >= 2:
                    evacuate(1, t - 2, tr2_done, 4)
            evacuate(1, 3, tr2_done, 4)
            evacuate(1, 4, tr2_done, 4)
            act.wait_ge(dl_ready, 1)
            nc.scalar.activation(ex[:, :, :], dl[:, :, :], ACT.Exp).then_inc(exp_done, 1)

            def gelu(i):
                c, j = steps[i]
                w = chunk_cols(c)[1]
                act.wait_ge(up_done, i + 1)
                if i >= RING:
                    act.wait_ge(gm_done, i - RING + 1)
                nc.scalar.activation(ge[:, i % RING, :w], bank[i % 2][:, :w], ACT.Gelu,
                                     bias=par_s[:, P_B1 + j:P_B1 + j + 1]).then_inc(gelu_done, 1)

            def high(i):
                w = chunk_cols(steps[i][0])[1]
                act.wait_ge(gm_done, i + 1)
                if i >= RING:
                    act.wait_ge(down_done, i - RING + 1)
                nc.scalar.activation(gmh[:, i % RING, :w], gm[:, i % RING, :w], ACT.Copy).then_inc(gmh_done, 1)

            for i in range(NS + 2):
                if i < NS:
                    gelu(i)
                if i >= 2:
                    high(i - 2)

        @block.vector
        def _(dve):
            v = nc.vector
            dve.wait_ge(spec_mm, 1)
            v.tensor_copy(spec_s[:, :, :], bank[5][:PF, :2 * D].rearrange("p (a d) -> p a d", a=2)).then_inc(spec_ev, 1)

            def stats(n, t, src):
                rows = TT[t][1]
                v.bn_stats(st[n][:rows, t, :], src[:rows, t, :]).then_inc(stat[n], 1)
                dve.wait_ge(stat[n], t + 1)
                v.bn_aggr(mv[n][:rows, t, :], st[n][:rows, t, :]).then_inc(var_ready[n], 1)

            def embed(t):
                rows = TT[t][1]
                dve.wait_ge(tok_done, t + 1)
                v.tensor_tensor(h_s[:rows, t, :], bank[t % 2][:rows, :D], tokb_s[:rows, :], ALU.add).then_inc(h_ready, 1)
                dve.wait_ge(h_ready, t + 1)
                stats(0, t, h_s)

            def normalise(n, t, src):
                rows = TT[t][1]
                dve.wait_ge(sd_ready[n], t + 1)
                v.reciprocal(rs[n][:rows, t:t + 1], sd[n][:rows, t:t + 1]).then_inc(rs_ready[n], 1)
                dve.wait_ge(rs_ready[n], t + 1)
                v.tensor_scalar(xn[n][:rows, t, :DA], src[:rows, t, :DA], mv[n][:rows, t, 0:1], rs[n][:rows, t:t + 1],
                                ALU.subtract, ALU.mult).then_inc(xn_ready[n], 1)
                v.tensor_scalar(xn[n][:rows, t, DA:].rearrange("p (a d) -> p a d", a=2),
                                src[:rows, t:t + 1, DA:].broadcast_to([rows, 2, DB]), mv[n][:rows, t, 0:1],
                                rs[n][:rows, t:t + 1], ALU.subtract, ALU.mult).then_inc(xn_ready[n], 1)

            def cut(n, t):
                s, rows = TT[t]
                c = slice(s, s + rows)
                dve.wait_ge(xt_ready[n], t + 1)
                v.tensor_copy(xth[n][:, :, c], xt32[n][:, :, c]).then_inc(hi_ready[n], 1)
                dve.wait_ge(hi_ready[n], t + 1)
                v.tensor_tensor(xtl[n][:, c], xt32[n][:, 0, c], xth[n][:, 0, c].bitcast(f32), ALU.subtract).then_inc(split[n], 1)
                v.tensor_tensor(xth[n][64:128, 1, c], xt32[n][64:128, 1, c], xth[n][64:128, 1, c].bitcast(f32),
                                ALU.subtract).then_inc(split[n], 1)

            dve.wait_ge(ld_sm, 16 * NSM)
            dve.wait_ge(ld_win, 32)
            for a in range(2):
                dve.wait_ge(win_hi, a + 1)
                v.tensor_tensor(win_l[:, a, :], win_s[:, a, :], win_h[:, a, :].bitcast(f32), ALU.subtract).then_inc(win_lo, 1)
            for t in range(NT):
                embed(t)
                if t >= 1:
                    normalise(0, t - 1, h_s)
                if t >= 3:
                    cut(0, t - 3)
            normalise(0, NT - 1, h_s)
            cut(0, 2)

            def project(p):
                dve.wait_ge(px_done, p + 1)
                v.tensor_tensor(xp_s[:, 2 * p:2 * p + 2, :], bank[4][:PTOK, :2 * D].rearrange("p (a d) -> p a d", a=2),
                                binx_s[:, None, :].broadcast_to([PTOK, 2, D]), ALU.add).then_inc(px_ev, 1)

            def spectrum(p):
                dve.wait_ge(fwd_done, p + 1)
                dve.wait_ge(spec_ev, 1)
                for k in range(2):
                    v.tensor_tensor(p_s[k][:, 2 * p:2 * p + 2, :], bank[5][:PF, :2 * D].rearrange("p (a d) -> p a d", a=2),
                                    spec_s[:, k:k + 1, :].broadcast_to([PF, 2, D]), ALU.mult).then_inc(spec_mul, 1)

            def short(h):
                im = slice(h * HIM, (h + 1) * HIM)
                for k, (xs, x, w) in enumerate(((xs_a, xt32[0][:, 0, :], P_WSA), (xs_b, xt32[0][0:DB, 1, :], P_WSB))):
                    rows = (DA, DB)[k]
                    xv = x.rearrange("p (b l) -> p b l", l=SEQ)[:, im, :]
                    sv = xs[:, :].rearrange("p (b l) -> p b l", l=SEQ)[:, im, :]
                    dve.wait_ge(xs_mid, 2 * h + k + 1)
                    v.scalar_tensor_tensor(sv[:, :, 1:], xv[:, :, :-1], par_s[0:rows, w:w + 1], sv[:, :, 1:],
                                           ALU.mult, ALU.add).then_inc(xs_step, 1)
                for k, (xs, x, w) in enumerate(((xs_a, xt32[0][:, 0, :], P_WSA), (xs_b, xt32[0][0:DB, 1, :], P_WSB))):
                    rows = (DA, DB)[k]
                    xv = x.rearrange("p (b l) -> p b l", l=SEQ)[:, im, :]
                    sv = xs[:, :].rearrange("p (b l) -> p b l", l=SEQ)[:, im, :]
                    dve.wait_ge(xs_step, 4 * h + k + 1)
                    v.scalar_tensor_tensor(sv[:, :, :-1], xv[:, :, 1:], par_s[0:rows, w + 2:w + 3], sv[:, :, :-1],
                                           ALU.mult, ALU.add).then_inc(xs_step, 1)

            def gates(h):
                b = [bank[6 + (5 * h + m) % 2] for m in range(5)]
                dve.wait_ge(silu_done, 2 * h + 2)
                v.scalar_tensor_tensor(u_b[:, h, :], b[1][64:128, :HALF], par_s[64:128, P_BZB:P_BZB + 1],
                                       zs_b[64:128, h, :], ALU.add, ALU.mult).then_inc(gate_done, 1)
                dve.wait_ge(gate_mm, 5 * h + 3)
                v.scalar_tensor_tensor(u_a[:, h, :], b[2][:, :HALF], par_s[:, P_BV1A:P_BV1A + 1],
                                       zs_a[:, h, :], ALU.add, ALU.mult).then_inc(gate_done, 1)
                dve.wait_ge(gate_mm, 5 * h + 4)
                dve.wait_ge(gate_done, 4 * h + 2)
                v.scalar_tensor_tensor(g_a[:, h, :], b[3][:, :HALF], par_s[:, P_BV2A:P_BV2A + 1],
                                       u_a[:, h, :], ALU.add, ALU.mult).then_inc(gate_done, 1)
                dve.wait_ge(gate_mm, 5 * h + 5)
                v.scalar_tensor_tensor(g_b[:, h, :], b[4][0:DB, :HALF], par_s[0:DB, P_BV2B:P_BV2B + 1],
                                       u_b[:, h, :], ALU.add, ALU.mult).then_inc(gate_done, 1)

            def mix(h):
                c = slice(h * HALF, (h + 1) * HALF)
                dve.wait_ge(gate_done, 4 * h + 4)
                dve.wait_ge(xs_step, 4 * h + 4)
                for k, (y, g, r) in enumerate(((y_a, g_a, DA), (y_b, g_b, DB))):
                    dve.wait_ge(inv_done, 2 * h + k + 1)
                    v.tensor_tensor(y[:, c], bank[k][:r, :HALF], g[:, h, :], ALU.mult).then_inc(y_done, 1)
                for k, (yt, y, xs) in enumerate(((yt_a, y_a, xs_a), (yt_b, y_b, xs_b))):
                    dve.wait_ge(y_done, 2 * h + k + 1)
                    v.tensor_tensor(yt[:, c], y[:, c], xs[:, c], ALU.add).then_inc(yt_done, 1)

            project(0)
            project(1)
            spectrum(0)
            gates(0)
            spectrum(1)
            cut(0, 3)
            cut(0, 4)
            short(0)
            project(2)
            project(3)
            mix(0)
            spectrum(2)
            spectrum(3)
            gates(1)
            short(1)

            def residual(t):
                rows = TT[t][1]
                dve.wait_ge(wo_done, t + 1)
                dve.wait_ge(hb_ready, t + 1)
                v.tensor_tensor(h2_s[:rows, t, :], bank[2 + t % 2][:rows, :D], hb_s[:rows, t, :], ALU.add).then_inc(h2_ready, 1)
                dve.wait_ge(h2_ready, t + 1)
                stats(1, t, h2_s)

            residual(0)
            residual(1)
            mix(1)
            normalise(1, 0, h2_s)
            for t in range(2, NT):
                residual(t)
                normalise(1, t - 1, h2_s)
                cut(1, t - 2)
            normalise(1, NT - 1, h2_s)
            cut(1, 3)
            cut(1, 4)

            def route():
                dve.wait_ge(lg_set, 1)
                for t in range(NT):
                    rows = TT[t][1]
                    dve.wait_ge(rt_done, t + 1)
                    v.tensor_tensor(lg[:rows, t, :], bank[6 + t % 2][:rows, :E], rb_s[:rows, :], ALU.add).then_inc(lg_ev, 1)
                for t in range(NT):
                    dve.wait_ge(lg_ev, t + 1)
                    v.max(mx[:, t, :], lg[:, t, :]).then_inc(mx_ready, 1)
                dve.wait_ge(mx_ready, NT)
                v.tensor_tensor(dl[:, :, :], lg[:, :, :], mx[:, :, 0:1].broadcast_to([128, NT, E]), ALU.subtract).then_inc(dl_ready, 1)
                for t in range(NT):
                    last = v.max_index(ix[:, t, :], mx[:, t, :], lg[:, t, :])
                last.then_inc(ix_ready, 1)
                dve.wait_ge(ix_ready, 1)
                v.tensor_copy(ixf[:, :, :], ix[:, :, 0:2]).then_inc(ix_ready, 1)
                dve.wait_ge(ix_ready, 2)
                iota = iota_s[:, None, :].broadcast_to([128, NT, E])
                v.tensor_tensor(m1[:, :, :], iota, ixf[:, :, 0:1].broadcast_to([128, NT, E]), ALU.is_equal).then_inc(best, 1)
                v.tensor_tensor(m2[:, :, :], iota, ixf[:, :, 1:2].broadcast_to([128, NT, E]), ALU.is_equal).then_inc(best, 1)
                dve.wait_ge(exp_done, 1)
                v.reduce_sum(se[:, :], ex[:, :, :], axis=AX.X).then_inc(sum_ready, 1)
                dve.wait_ge(best, 2)
                v.tensor_tensor(mk[:, :, :], m1[:, :, :], m2[:, :, :], ALU.add).then_inc(best, 1)
                dve.wait_ge(sum_ready, 1)
                v.reciprocal(re[:, :], se[:, :]).then_inc(sum_ready, 1)
                dve.wait_ge(best, 3)
                v.tensor_tensor(em[:, :, :], ex[:, :, :], mk[:, :, :], ALU.mult).then_inc(best, 1)
                dve.wait_ge(best, 4)
                dve.wait_ge(sum_ready, 2)
                v.tensor_tensor(gt[:, :, :], em[:, :, :], re[:, :, None].broadcast_to([128, NT, E]), ALU.mult).then_inc(ghl_ready, 1)
                dve.wait_ge(ghl_ready, 1)
                v.tensor_copy(ghl[:, :, 0:E].bitcast(f32r), gt[:, :, :]).then_inc(ghl_ready, 1)
                dve.wait_ge(ghl_ready, 2)
                v.tensor_tensor(ghl[:, :, E:2 * E], gt[:, :, :], ghl[:, :, 0:E], ALU.subtract).then_inc(ghl_ready, 1)
                for c in range(len(CHUNKS)):
                    s, cols = chunk_cols(c)
                    dve.wait_ge(gtr_done, c + 1)
                    v.tensor_copy(gT[:, s:s + cols], bank[6 + c][:2 * E, :cols]).then_inc(gT_ready, 1)

            route()

            def weigh(i):
                w = chunk_cols(steps[i][0])[1]
                dve.wait_ge(gelu_done, i + 1)
                dve.wait_ge(gb_done, i + 1)
                v.tensor_tensor(gm[:, i % RING, :w], bank[2 + i % 2][:, :w], ge[:, i % RING, :w], ALU.mult).then_inc(gm_done, 1)

            def low(i):
                w = chunk_cols(steps[i][0])[1]
                dve.wait_ge(gmh_done, i + 1)
                v.tensor_tensor(gml[:, i % RING, :w], gm[:, i % RING, :w], gmh[:, i % RING, :w].bitcast(f32),
                                ALU.subtract).then_inc(gml_done, 1)

            def finish(c):
                for k, t in enumerate(CHUNKS[c]):
                    rows = TT[t][1]
                    if k < len(CHUNKS[c]) - 1:
                        dve.wait_ge(acc_done, t + 1 - c)
                    else:
                        dve.wait_ge(down_done, (c + 1) * HC)
                    v.tensor_tensor(o_s[:rows, t, :], bank[4 + k][:rows, :D], h2_s[:rows, t, :], ALU.add).then_inc(fin_done, 1)

            for i in range(NS + 2):
                if i < NS:
                    weigh(i)
                if i >= 2:
                    low(i - 2)
                if i == HC + DOWN_LAG - G_LAG:
                    finish(0)
            finish(1)

        @block.tensor
        def _(pe):
            mm = nc.tensor.matmul

            def five(dst, rows, cols, n, w_h, w_l, x_side, start=True, stop=True):
                terms = ((xth[n][:, 0], w_h[:, 0]), (xth[n][:, 0], w_l[:, 0]), (xtl[n], w_h[:, 0]),
                         (xth[n][:, 1], w_h[:, 1]), (xth[n][:, 1], w_l[:, 1]))
                for k, (x, w) in enumerate(terms):
                    a, b = x[:, rows], w[:, cols]
                    if x_side == "moving":
                        a, b = b, a
                    last = mm(dst, a, b, start=start and k == 0, stop=stop and k == len(terms) - 1)
                return last

            pe.wait_ge(ld_cst, 16 * NCST)
            for k in range(2):
                last = mm(bank[5][:PF, k * D:(k + 1) * D], basis_s[:, k, :], waug_s[:, :], start=True, stop=True)
            last.then_inc(spec_mm, 1)

            def embed(t):
                s, n = TT[t]
                pe.wait_ge(ld_x[t], 16)
                if t >= 2:
                    pe.wait_ge(h_ready, t - 1)
                for k in range(KP):
                    last = mm(bank[t % 2][:n, :D], x_s[:, KP * s + k * n:KP * s + (k + 1) * n], tokw_s[:, k, :],
                              start=k == 0, stop=k == KP - 1)
                last.then_inc(tok_done, 1)

            def transpose(n, t, banks, done):
                rows = TT[t][1]
                pe.wait_ge(xn_ready[n], 2 * t + 2)
                if t >= 2:
                    pe.wait_ge(xt_ready[n], t - 1)
                b = bank[banks + t % 2]
                nc.tensor.transpose(b[:, 0:rows], xn[n][:rows, t, 0:DA], ident_s[:rows, :rows])
                nc.tensor.transpose(b[:, 128:128 + rows], xn[n][:rows, t, DA:], ident_s[:rows, :rows]).then_inc(done, 1)

            pe.wait_ge(ld_tokw, 16)
            for t in range(NT):
                embed(t)
                if t >= 2:
                    transpose(0, t - 2, 2, tr_done)

            def project(p):
                pe.wait_ge(split[0], 2 * (tile_of((2 * p + 2) * PTOK - 1) + 1))
                if p == 0:
                    pe.wait_ge(win_lo, 2)
                else:
                    pe.wait_ge(px_ev, p)
                for q in range(2):
                    g = 2 * p + q
                    last = five(bank[4][:PTOK, q * D:(q + 1) * D], slice(g * PTOK, (g + 1) * PTOK), slice(0, D), 0,
                                win_h, win_l, "stationary")
                last.then_inc(px_done, 1)

            def forward(p):
                pe.wait_ge(px_ev, p + 1)
                if p == 0:
                    pe.wait_ge(spec_ev, 1)
                else:
                    pe.wait_ge(spec_mul, 2 * p)
                mm(bank[5][:PF, :2 * D], fwd_s[:, :], xp_s[:, 2 * p:2 * p + 2, :], start=True, stop=True).then_inc(fwd_done, 1)

            def gate(h, m):
                i = 5 * h + m
                if i >= 2:
                    j = i - 2
                    if j % 5 == 0:
                        pe.wait_ge(silu_done, 2 * (j // 5) + 1)
                    else:
                        pe.wait_ge(gate_done, 4 * (j // 5) + j % 5)
                c0, w = GATE_COL[m]
                five(bank[6 + i % 2][:w, :HALF], slice(h * HALF, (h + 1) * HALF), slice(c0, c0 + w), 0,
                     win_h, win_l, "moving").then_inc(gate_mm, 1)

            def inverse(h):
                pe.wait_ge(spec_mul, 4 * (h + 1))
                if h == 0:
                    pe.wait_ge(h_ready, NT)
                else:
                    pe.wait_ge(y_done, 2)
                for k, (d0, d1) in enumerate(((0, DA), (DA, D))):
                    for g in range(PAIRS // 2):
                        for part in range(2):
                            last = mm(bank[k][:d1 - d0, g * PTOK:(g + 1) * PTOK], p_s[part][:, h * PAIRS // 2 + g, d0:d1],
                                      inv_s[:, part, :], start=part == 0, stop=part == 1)
                    last.then_inc(inv_done, 1)

            def merge(t):
                s, n = TT[t]
                pe.wait_ge(yt_done, 2 * ((s + n - 1) // HALF + 1))
                if t < 2:
                    pe.wait_ge(xt_ready[0], NT)
                    pe.wait_ge(ld_wo, 32)
                else:
                    pe.wait_ge(h2_ready, t - 1)
                b = bank[2 + t % 2][:n, :D]
                mm(b, yt_a[:, s:s + n], woa_s[:, :], start=True, stop=False)
                mm(b, yt_b[:, s:s + n], wob_s[:, :], start=False, stop=True).then_inc(wo_done, 1)

            def logits(t):
                s, n = TT[t]
                pe.wait_ge(split[1], 2 * (t + 1))
                if t == 0:
                    pe.wait_ge(sm_lo, 2)
                    pe.wait_ge(gate_done, 8)
                if t >= 2:
                    pe.wait_ge(lg_ev, t - 1)
                five(bank[6 + t % 2][:n, :E], slice(s, s + n), slice(0, E), 1, rw_h, rw_l, "stationary").then_inc(rt_done, 1)

            project(0)
            project(1)
            gate(0, 0)
            forward(0)
            gate(0, 1)
            gate(0, 2)
            gate(0, 3)
            forward(1)
            gate(0, 4)
            transpose(0, 3, 2, tr_done)
            transpose(0, 4, 2, tr_done)
            project(2)
            project(3)
            inverse(0)
            gate(1, 0)
            forward(2)
            gate(1, 1)
            gate(1, 2)
            forward(3)
            merge(0)
            merge(1)
            gate(1, 3)
            gate(1, 4)
            inverse(1)
            for t in range(2, NT):
                transpose(1, t - 2, 4, tr2_done)
                merge(t)
            transpose(1, 3, 4, tr2_done)
            transpose(1, 4, 4, tr2_done)
            for t in range(NT):
                logits(t)

            def gates_across(c):
                pe.wait_ge(ghl_ready, 3)
                s0 = chunk_cols(c)[0]
                for t in CHUNKS[c]:
                    s, n = TT[t]
                    last = nc.tensor.transpose(bank[6 + c][:2 * E, s - s0:s - s0 + n], ghl[:n, t, :], ident_s[:n, :n])
                last.then_inc(gtr_done, 1)

            def up(i):
                c, j = steps[i]
                s, w = chunk_cols(c)
                if i == 0:
                    pe.wait_ge(y_done, 4)
                if i >= 2:
                    pe.wait_ge(gelu_done, i - 1)
                if c == 0 and j % 3 == 0:
                    pe.wait_ge(w1_lo, j // 3 + 1)
                five(bank[i % 2][:, :w], slice(s, s + w), slice(j * 128, (j + 1) * 128), 1, w1_h, w1_l,
                     "moving").then_inc(up_done, 1)

            def spread(i):
                c, j = steps[i]
                s, w = chunk_cols(c)
                if i == 0:
                    pe.wait_ge(ld_sel, 16)
                    pe.wait_ge(h2_ready, NT)
                if j == 0:
                    pe.wait_ge(gT_ready, c + 1)
                if i >= 2:
                    pe.wait_ge(gm_done, i - 1)
                mm(bank[2 + i % 2][:, :w], sel_r[:, j * 128:(j + 1) * 128], gT[:, s:s + w], start=True,
                   stop=True).then_inc(gb_done, 1)

            def down(i):
                c, j = steps[i]
                s0 = chunk_cols(c)[0]
                pe.wait_ge(gmh_done, i + 1)
                pe.wait_ge(gml_done, i + 1)
                if c == 0 and j % 3 == 0:
                    pe.wait_ge(w2_lo, j // 3 + 1)
                if j == 0:
                    if c == 0:
                        pe.wait_ge(xt_ready[1], NT)
                        pe.wait_ge(gT_ready, len(CHUNKS))
                    else:
                        pe.wait_ge(fin_done, len(CHUNKS[0]))
                r = i % RING
                for k, t in enumerate(CHUNKS[c]):
                    s, n = TT[t]
                    acc = bank[4 + k][:n, :D]
                    rows = slice(s - s0, s - s0 + n)
                    if j == 0:
                        mm(acc, gT[:, s:s + n], b2_h[:, :], start=True, stop=False)
                        mm(acc, gT[:, s:s + n], b2_l[:, :], start=False, stop=False)
                    mm(acc, gmh[:, r, rows], w2_h[:, j, :], start=False, stop=False)
                    mm(acc, gmh[:, r, rows], w2_l[:, j, :], start=False, stop=False)
                    last = mm(acc, gml[:, r, rows], w2_h[:, j, :], start=False, stop=j == HC - 1)
                    if j == HC - 1 and k < len(CHUNKS[c]) - 1:
                        last.then_inc(acc_done, 1)
                last.then_inc(down_done, 1)

            for i in range(NS + DOWN_LAG):
                if i < NS:
                    up(i)
                if i == 1:
                    for c in range(len(CHUNKS)):
                        gates_across(c)
                if 0 <= i - G_LAG < NS:
                    spread(i - G_LAG)
                if i >= DOWN_LAG:
                    down(i - DOWN_LAG)


def constants():
    import numpy as np
    k = np.arange(SEQ)
    f_cos, f_sin = np.arange(POINTS // 2 + 1), np.arange(1, POINTS // 2)
    turn = 2 * np.pi / POINTS
    trig = np.concatenate([np.cos(turn * np.outer(f_cos, k)), np.sin(turn * np.outer(f_sin, k))])
    pos = np.sin(np.outer(k, np.arange(TAPS)) / TAPS)
    pos = np.concatenate([pos, np.ones((SEQ, 1))], 1)
    f_all = np.concatenate([f_cos, f_sin])
    basis = np.stack([np.cos(turn * np.outer(f_all, k)) @ pos, np.sin(turn * np.outer(f_all, k)) @ pos])
    basis = np.concatenate([basis, basis], 1).transpose(2, 0, 1)
    fwd = np.zeros((PTOK, PF))
    inv = np.zeros((PF, 2, PTOK))
    theta = turn * np.outer(f_all, k - SEQ // 2)
    weight = np.where((f_all == 0) | (f_all == POINTS // 2), 1.0, 2.0)[:, None] / POINTS
    is_cos = (np.arange(POINTS) < len(f_cos))[:, None]
    first = weight * np.where(is_cos, np.cos(theta), np.sin(theta))
    second = weight * np.where(is_cos, -np.sin(theta), np.cos(theta))
    for b in range(2):
        rows, cols = slice(b * SEQ, (b + 1) * SEQ), slice(b * POINTS, (b + 1) * POINTS)
        fwd[rows, cols] = trig.T
        inv[cols, 0, rows] = first
        inv[cols, 1, rows] = second
    expert = np.arange(HC * 128) // HID
    sel = np.tile((np.arange(E)[:, None] == expert[None, :]), (2, 1))
    made = dict(c_basis=basis, c_fwd=fwd, c_inv=inv, c_sel=sel, c_ident=np.eye(128), c_iota=np.arange(E))
    return {n: np.ascontiguousarray(a, dtype=np.float32) for n, a in made.items()}


def kernel(x, L0_tok_W, L0_tok_b, L0_attn_w_in, L0_attn_b_in, L0_attn_w_filt, L0_attn_b_filt,
           L0_attn_w_short, L0_attn_b_short, L0_attn_w_out, L0_attn_b_out, L0_ffn_router_w,
           L0_ffn_router_b, L0_ffn_w1, L0_ffn_b1, L0_ffn_w2, L0_ffn_b2):
    import numpy as np
    import concourse.bacc as bacc
    from concourse.bass_utils import run_bass_kernel_spmd

    def split_rows(w, twice):
        return w[:DA], np.concatenate([w[DA:], w[DA:]]) if twice else w[DA:]

    a = {k: np.asarray(v) for k, v in locals().items() if k == "x" or k.startswith("L0_")}
    patches = a["x"].reshape(IMAGES, 3, 6, 16, 6, 16).transpose(1, 3, 5, 0, 2, 4).reshape(KP, 128, TOK)
    xt = np.concatenate([patches[:, :, s:s + n].transpose(1, 0, 2).reshape(128, KP * n) for s, n in TT], 1)
    order = np.concatenate([np.arange(0, D), D + np.arange(DA), D + np.arange(DA, D), 2 * D + np.arange(DA, D),
                            2 * D + np.arange(DA), 3 * D + np.arange(DA), 3 * D + np.arange(DA, D)])
    win_a, win_b = split_rows(a["L0_attn_w_in"][:, order], True)
    b_in, w_short, b_short = a["L0_attn_b_in"], a["L0_attn_w_short"][:, 0, :], a["L0_attn_b_short"]
    par = np.zeros((128, NPAR), np.float32)
    par[:, P_BZA] = b_in[D:D + DA]
    par[:, P_BZB] = np.concatenate([b_in[D + DA:2 * D], b_in[2 * D + DA:3 * D]])
    par[:, P_BV1A] = b_in[2 * D:2 * D + DA]
    par[:, P_BV2A] = b_in[3 * D:3 * D + DA]
    par[:DB, P_BV2B] = b_in[3 * D + DA:]
    par[:, P_WSA:P_WSA + 3] = w_short[:DA]
    par[:DB, P_WSB:P_WSB + 3] = w_short[DA:]
    par[:, P_BSA] = b_short[:DA]
    par[:DB, P_BSB] = b_short[DA:]
    par[:, P_B1:] = a["L0_ffn_b1"].reshape(HC, 128).T
    wo_a, wo_b = split_rows(a["L0_attn_w_out"], False)
    rw_a, rw_b = split_rows(a["L0_ffn_router_w"], True)
    w1 = np.stack(split_rows(a["L0_ffn_w1"].transpose(1, 0, 2).reshape(D, HC * 128), True), 1)
    w1 = w1.reshape(128, 2, PIECES, W1P).transpose(0, 2, 1, 3).reshape(128, PIECES, 2 * W1P)
    arrays = dict(
        xt=xt, tokw=a["L0_tok_W"].T.reshape(KP, 128, D).transpose(1, 0, 2), tokb=a["L0_tok_b"],
        win_a=win_a, win_b=win_b, binx=b_in[:D], par=par, wo_a=wo_a, wo_b=wo_b, bout=a["L0_attn_b_out"],
        waug=np.concatenate([a["L0_attn_w_filt"], a["L0_attn_b_filt"][None]]), rw_a=rw_a, rw_b=rw_b,
        rb=a["L0_ffn_router_b"], w1=w1,
        w2=a["L0_ffn_w2"].reshape(HC, 128, D).transpose(1, 0, 2).reshape(128, PIECES, W2P * D), b2=np.concatenate([a["L0_ffn_b2"]] * 2),
        **constants())
    arrays = {k: np.ascontiguousarray(v) for k, v in arrays.items()}
    nc = bacc.Bacc("TRN2", target_bir_lowering=False, num_devices=1)
    args = [nc.dram_tensor(k, v.shape, mybir.dt.from_np(v.dtype), kind="ExternalInput").ap() for k, v in arrays.items()]
    out = nc.dram_tensor("out", (TOK, D), mybir.dt.float32, kind="ExternalOutput").ap()
    build(nc, *args, out)
    r = run_bass_kernel_spmd(nc, [arrays], core_ids=[0])
    return r.results[0]["out"].reshape(IMAGES, SEQ, D)
```

```python
import math

import concourse.bass as bass
from concourse import mybir
from contextlib import ExitStack

D = 192
DA, DB = 128, 64
IMAGES, SEQ = 16, 36
TOK = IMAGES * SEQ
TT = [(s, min(128, TOK - s)) for s in range(0, TOK, 128)]
NT = len(TT)
PIX = 768
KP = PIX // 128
PAIRS = IMAGES // 2
PTOK = 2 * SEQ
POINTS = 54
PF = 2 * POINTS
HALF = TOK // 2
HIM = IMAGES // 2
TAPS = 64
E = 8
HID = 288
HC = E * HID // 128
GATE_COL = [(192, 128), (320, 128), (448, 128), (576, 128), (704, 64)]
P_BZA, P_BZB, P_BV1A, P_BV2A, P_BV2B, P_WSA, P_WSB, P_BSA, P_BSB, P_B1 = 0, 1, 2, 3, 4, 5, 8, 11, 12, 13
NPAR = P_B1 + HC
CHUNKS = [(0, 1), (2, 3, 4)]
EPS = 1e-5
LN2_STEP = 6
PIECES = 6
W1P = HC * 128 // PIECES
W2P = HC // PIECES
WARM = 11
RING = 5
G_LAG, DOWN_LAG = 1, 4


ROWS128 = dict(ident=128, tokb=D, par=NPAR, iota=E, rb=E, rw=2 * E)
ROWS65 = dict(waug=D, basis=2 * PF)
ROWS108 = dict(fwd=PF, inv=2 * PTOK)
LATE128 = dict(wo_a=D, wo_b=D, bout=D)


def columns(pack):
    at, found = 0, {}
    for name, width in pack.items():
        found[name] = slice(at, at + width)
        at += width
    return found


def build(nc, xt, tokw, win, binx, rows128, rows65, rows108, late128, b2, w1, w2, c_sel, out):
    f32, f32r, u32 = mybir.dt.float32, mybir.dt.float32r, mybir.dt.uint32
    ALU, ACT, AX = mybir.AluOpType, mybir.ActivationFunctionType, mybir.AxisListType
    ctx = ExitStack()
    with ctx:
        def sb(name, shape, dt=f32):
            return ctx.enter_context(nc.sbuf_tensor(name, shape, dt))

        def sem(name):
            return ctx.enter_context(nc.semaphore(name))

        x_s = sb("x_s", [128, KP * TOK])
        tokw_s = sb("tokw_s", [128, KP, D])
        win_s = sb("win_s", [128, 2, 4 * D])
        win_h = sb("win_h", [128, 2, 4 * D], f32r)
        win_l = sb("win_l", [128, 2, 4 * D], f32r)
        pk128 = sb("pk128", [128, sum(ROWS128.values())])
        pk65 = sb("pk65", [TAPS + 1, sum(ROWS65.values())])
        pk108 = sb("pk108", [PF, sum(ROWS108.values())])
        pkl = sb("pkl", [128, sum(LATE128.values())])
        at = columns(ROWS128)
        ident_s, tokb_s, par_s, iota_s, rb_s = (pk128[:, at[n]] for n in ("ident", "tokb", "par", "iota", "rb"))
        rw_s = pk128[:, at["rw"]].rearrange("p (a e) -> p a e", a=2)
        at = columns(ROWS65)
        waug_s = pk65[:, at["waug"]]
        basis_s = pk65[:, at["basis"]].rearrange("p (a r) -> p a r", a=2)
        at = columns(ROWS108)
        fwd_s = pk108[:PTOK + 1, at["fwd"]]
        inv_s = pk108[:, at["inv"]].rearrange("p (a t) -> p a t", a=2)
        at = columns(LATE128)
        woa_s, wob_s, bout_s = pkl[:, at["wo_a"]], pkl[:DB, at["wo_b"]], pkl[:, at["bout"]]
        rw_h = sb("rw_h", [128, 2, E], f32r)
        rw_l = sb("rw_l", [128, 2, E], f32r)
        stage = sb("stage", [128, PIECES, 2 * W1P])
        w1_h = sb("w1_h", [128, 2, HC * 128], f32r)
        w1_l = sb("w1_l", [128, 2, HC * 128], f32r)
        w2_h = sb("w2_h", [128, HC, D], f32r)
        w2_l = sb("w2_l", [128, HC, D], f32r)
        b2_s = sb("b2_s", [2 * E, D])
        b2_h = sb("b2_h", [2 * E, D], f32r)
        b2_l = sb("b2_l", [2 * E, D], f32r)
        sel_r = sb("sel_r", [2 * E, HC * 128], f32r)
        eps_s = sb("eps_s", [128, 1])
        minus_half = sb("minus_half", [128, 1])
        euler = sb("euler", [128, E * len(CHUNKS[-1])])
        idle = sb("idle", [128, 512], mybir.dt.bfloat16)
        h_s = sb("h_s", [128, NT, D])
        hb_s = sb("hb_s", [128, NT, D])
        h2_s = sb("h2_s", [128, NT, D])
        o_s = h_s
        st = [sb(f"st{n}", [128, NT, 6]) for n in range(2)]
        mv = [sb(f"mv{n}", [128, NT, 2]) for n in range(2)]
        sd = [sb(f"sd{n}", [128, NT]) for n in range(2)]
        rs = [sb(f"rs{n}", [128, NT]) for n in range(2)]
        xn = [sb("xn", [128, NT, 2 * DA])] * 2
        xt32 = [sb("xt32", [128, 2, TOK])] * 2
        xth = [sb("xth", [128, 2, TOK], f32r)] * 2
        xtl = [sb("xtl", [128, TOK], f32r)] * 2
        spec_s = sb("spec_s", [PF, 2, D])
        xp_s = win_s[:PTOK + 1, :, :].rearrange("p a n -> p (a n)").rearrange("p (g d) -> p g d", d=D)
        p_s = [x_s[:PF, n * PAIRS * D:(n + 1) * PAIRS * D].rearrange("p (g d) -> p g d", d=D) for n in range(2)]
        zs_a = sb("zs_a", [DA, 2, HALF])
        zs_b = sb("zs_b", [128, 2, HALF])
        u_a = g_a = zs_a
        u_b = sb("u_b", [DB, 2, HALF])
        g_b = u_b
        xs_a = sb("xs_a", [DA, TOK])
        xs_b = sb("xs_b", [DB, TOK])
        yt_a = y_a = sb("y_a", [DA, TOK])
        yt_b = y_b = sb("y_b", [DB, TOK])
        lg = sb("lg", [128, NT, E])
        mx = sb("mx", [128, NT, E])
        ix = sb("ix", [128, NT, E], u32)
        ixf = sb("ixf", [128, NT, 2])
        dl = sb("dl", [128, NT, E])
        ex = sb("ex", [128, NT, E])
        m1 = sb("m1", [128, NT, E])
        m2 = sb("m2", [128, NT, E])
        mk = sb("mk", [128, NT, E])
        em = sb("em", [128, NT, E])
        se = sb("se", [128, NT])
        re = sb("re", [128, NT])
        gt = sb("gt", [128, NT, E])
        ghl = sb("ghl", [128, NT, 2 * E])
        gT = sb("gT", [2 * E, TOK], f32r)
        CW = max(sum(TT[t][1] for t in ts) for ts in CHUNKS)
        ge, gm = (x_s[:, n * RING * CW:(n + 1) * RING * CW].rearrange("p (r c) -> p r c", c=CW) for n in range(2))
        gmh = sb("gmh", [128, RING, CW], f32r)
        gml = sb("gml", [128, RING, CW], f32r)

        bank = [ctx.enter_context(nc.psum_tensor(f"bank{i}", [128, 512], f32)) for i in range(8)]

        ld_tokw, ld_win, ld_128, ld_65, ld_108, ld_late, ld_b2, ld_binx, ld_sel, stored = map(
            sem, ["ld_tokw", "ld_win", "ld_128", "ld_65", "ld_108", "ld_late", "ld_b2", "ld_binx", "ld_sel", "stored"])
        ld_w1, ld_w2 = ([sem(f"ld_{n}_{q}") for q in range(PIECES)] for n in ("w1", "w2"))
        ld_x = [sem(f"ld_x{t}") for t in range(NT)]
        tok_done, spec_mm, tr_done, px_done, fwd_done, gate_mm, inv_done, wo_done = map(
            sem, ["tok_done", "spec_mm", "tr_done", "px_done", "fwd_done", "gate_mm", "inv_done", "wo_done"])
        tr2_done, rt_done, gtr_done, up_done, gb_done, down_done, acc_done = map(
            sem, ["tr2_done", "rt_done", "gtr_done", "up_done", "gb_done", "down_done", "acc_done"])
        win_hi, w1_hi, w2_hi, sm_hi, win_lo, w1_lo, w2_lo, sm_lo = map(
            sem, ["win_hi", "w1_hi", "w2_hi", "sm_hi", "win_lo", "w1_lo", "w2_lo", "sm_lo"])
        idle_set, powers_set = sem("idle_set"), sem("powers_set")
        eps_set, lg_set, spec_ev, h_ready, hb_ready, h2_ready = map(
            sem, ["eps_set", "lg_set", "spec_ev", "h_ready", "hb_ready", "h2_ready"])
        stat, var_ready, sd_ready, rs_ready, xn_ready, xt_ready, hi_ready, split = (
            [sem(f"{n}{k}") for k in (1, 2)] for n in
            ("stat", "var_ready", "sd_ready", "rs_ready", "xn_ready", "xt_ready", "hi_ready", "split"))
        px_ev, spec_mul, silu_done, gate_done, xs_mid, xs_step, y_done, yt_done = map(
            sem, ["px_ev", "spec_mul", "silu_done", "gate_done", "xs_mid", "xs_step", "y_done", "yt_done"])
        lg_ev, mx_ready, dl_ready, ix_ready, best, exp_done, sum_ready, ghl_ready, gT_ready = map(
            sem, ["lg_ev", "mx_ready", "dl_ready", "ix_ready", "best", "exp_done", "sum_ready", "ghl_ready", "gT_ready"])
        gelu_done, gm_done, gmh_done, gml_done, fin_done = map(
            sem, ["gelu_done", "gm_done", "gmh_done", "gml_done", "fin_done"])

        steps = [(c, j) for c in range(len(CHUNKS)) for j in range(HC)]
        NS = len(steps)

        def chunk_cols(c):
            s = TT[CHUNKS[c][0]][0]
            return s, sum(TT[t][1] for t in CHUNKS[c])

        def piece1(q):
            return stage[:, q, :].rearrange("p (a n) -> p a n", a=2)

        def piece2(q):
            return stage[:, q, :W2P * D].rearrange("p (j d) -> p j d", d=D)

        def tile_of(token):
            return token // 128

        block = ctx.enter_context(nc.Block())

        @block.sync
        def _(sp):
            def load_x(t):
                s, n = TT[t]
                sp.dma_start(x_s[:, KP * s:KP * (s + n)], xt[:, KP * s:KP * (s + n)]).then_inc(ld_x[t], 16)

            load_x(0)
            load_x(1)
            load_x(2)
            sp.dma_start(win_s[:, :, :], win).then_inc(ld_win, 16)
            load_x(3)
            load_x(4)
            for q in range(PIECES):
                sp.dma_start(stage[:, q, :], w1[:, q, :]).then_inc(ld_w1[q], 16)
            sp.wait_ge(win_lo, 2)
            sp.dma_start(xp_s[PTOK:PTOK + 1, :, :], binx.partition_broadcast(PAIRS).rearrange("(o g) d -> o g d", o=1)).then_inc(ld_binx, 16)
            for q in range(PIECES):
                sp.wait_ge(w1_lo, q + 1)
                sp.dma_start(stage[:, q, :W2P * D], w2[:, q, :]).then_inc(ld_w2[q], 16)
            for t, (s, n) in enumerate(TT):
                sp.wait_ge(fin_done, t + 1)
                sp.dma_start(out[s:s + n, :], o_s[:n, t, :]).then_inc(stored, 16)
            sp.wait_ge(stored, 16 * NT)

        @block.gpsimd
        def _(pool):
            g = nc.gpsimd
            g.memset(eps_s[:, :], EPS).then_inc(eps_set, 1)
            g.memset(lg[:, :, :], 0.0).then_inc(lg_set, 1)
            g.memset(minus_half[:, :], -0.5)
            g.memset(euler[:, :], math.e).then_inc(powers_set, 1)
            pool.dma_start(sel_r[:, :], c_sel).then_inc(ld_sel, 16)

            def low_w1(q):
                pool.wait_ge(w1_hi, q + 1)
                c = slice(q * W1P, (q + 1) * W1P)
                g.tensor_tensor(w1_l[:, :, c], piece1(q), w1_h[:, :, c].bitcast(f32), ALU.subtract).then_inc(w1_lo, 1)

            def low_w2(q):
                pool.wait_ge(w2_hi, q + 1)
                c = slice(q * W2P, (q + 1) * W2P)
                g.tensor_tensor(w2_l[:, c, :], piece2(q), w2_h[:, c, :].bitcast(f32), ALU.subtract).then_inc(w2_lo, 1)

            def with_bias(t):
                rows = TT[t][1]
                pool.wait_ge(h_ready, t + 1)
                g.tensor_tensor(hb_s[:rows, t, :], h_s[:rows, t, :], bout_s[:rows, :], ALU.add).then_inc(hb_ready, 1)

            pool.wait_ge(sm_hi, 2)
            g.tensor_tensor(rw_l[:, :, :], rw_s, rw_h[:, :, :].bitcast(f32), ALU.subtract).then_inc(sm_lo, 1)
            g.tensor_tensor(b2_l[:, :], b2_s[:, :], b2_h[:, :].bitcast(f32), ALU.subtract).then_inc(sm_lo, 1)
            for q in range(PIECES):
                low_w1(q)
            pool.wait_ge(ld_late, 16)
            with_bias(0)
            with_bias(1)

            def inverse_deviation(t):
                rows = TT[t][1]
                pool.wait_ge(var_ready[1], 2 * t + 2)
                g.tensor_tensor(rs[1][:rows, t:t + 1], mv[1][:rows, t, 1:2], minus_half[:rows, :], ALU.pow).then_inc(rs_ready[1], 1)

            def exponentials(c):
                ts = CHUNKS[c]
                w = slice(ts[0], ts[-1] + 1)
                pool.wait_ge(dl_ready, c + 1)
                g.tensor_tensor(ex[:, w, :], euler[:, :len(ts) * E].rearrange("p (t e) -> p t e", e=E), dl[:, w, :], ALU.pow).then_inc(exp_done, 1)

            pool.wait_ge(powers_set, 1)
            low_w2(0)
            low_w2(1)
            with_bias(2)
            with_bias(3)
            with_bias(4)
            inverse_deviation(0)
            inverse_deviation(1)
            low_w2(2)
            exponentials(0)
            low_w2(3)
            inverse_deviation(2)
            inverse_deviation(3)
            inverse_deviation(4)
            low_w2(4)
            low_w2(5)
            exponentials(1)

        @block.scalar
        def _(act):
            act.dma_start(tokw_s[:, :, :], tokw).then_inc(ld_tokw, 16)
            act.dma_start(pk128[:, :], rows128).then_inc(ld_128, 16)
            act.dma_start(pk65[:, :], rows65).then_inc(ld_65, 16)
            act.dma_start(pk108[:, :], rows108).then_inc(ld_108, 16)
            act.dma_start(b2_s[:, :], b2).then_inc(ld_b2, 16)
            act.dma_start(pkl[:, :], late128).then_inc(ld_late, 16)

            def cut_high(dst, src, done):
                nc.scalar.activation(dst, src, ACT.Copy).then_inc(done, 1)

            def deviation(t):
                rows = TT[t][1]
                act.wait_ge(var_ready[0], t + 1)
                nc.scalar.activation(sd[0][:rows, t:t + 1], mv[0][:rows, t, 1:2], ACT.Sqrt,
                                     bias=eps_s[:rows, :]).then_inc(sd_ready[0], 1)

            def high_w1(q):
                act.wait_ge(ld_w1[q], 16)
                cut_high(w1_h[:, :, q * W1P:(q + 1) * W1P], piece1(q), w1_hi)

            def high_w2(q):
                act.wait_ge(ld_w2[q], 16)
                cut_high(w2_h[:, q * W2P:(q + 1) * W2P, :], piece2(q), w2_hi)

            def evacuate(n, t, done, b):
                s, rows = TT[t]
                act.wait_ge(done, t + 1)
                src = bank[b][:, 0:256].rearrange("p (a c) -> p a c", a=2)[:, :, :rows]
                nc.scalar.activation(xt32[n][:, :, s:s + rows], src, ACT.Copy).then_inc(xt_ready[n], 1)

            act.wait_ge(eps_set, 1)
            act.wait_ge(ld_win, 16)
            cut_high(win_h[:, 0, :], win_s[:, 0, :], win_hi)
            deviation(0)
            cut_high(win_h[:, 1, :], win_s[:, 1, :], win_hi)
            deviation(1)
            evacuate(0, 0, tr_done, 2)
            deviation(2)
            evacuate(0, 1, tr_done, 3)
            act.wait_ge(ld_128, 16)
            act.wait_ge(ld_b2, 16)
            cut_high(rw_h[:, :, :], rw_s, sm_hi)
            cut_high(b2_h[:, :], b2_s[:, :], sm_hi)
            high_w1(0)
            deviation(3)
            evacuate(0, 2, tr_done, 2)
            high_w1(1)
            high_w1(2)
            deviation(4)

            def short_mid(h):
                act.wait_ge(xt_ready[0], (3, NT)[h])
                c = slice(h * HALF, (h + 1) * HALF)
                nc.scalar.activation(xs_a[:, c], xt32[0][:, 0, c], ACT.Identity, bias=par_s[:, P_BSA:P_BSA + 1],
                                     scale=par_s[:, P_WSA + 1:P_WSA + 2]).then_inc(xs_mid, 1)
                nc.scalar.activation(xs_b[:, c], xt32[0][0:DB, 1, c], ACT.Identity, bias=par_s[0:DB, P_BSB:P_BSB + 1],
                                     scale=par_s[0:DB, P_WSB + 1:P_WSB + 2]).then_inc(xs_mid, 1)

            def project(p):
                act.wait_ge(px_done, p + 1)
                nc.scalar.activation(xp_s[:PTOK, 2 * p:2 * p + 2, :], bank[4][:PTOK, :2 * D].rearrange("p (a d) -> p a d", a=2),
                                     ACT.Copy).then_inc(px_ev, 1)

            def silus(h):
                act.wait_ge(gate_mm, 5 * h + 1)
                nc.scalar.activation(zs_a[:, h, :], bank[6 + (5 * h) % 2][:, :HALF], ACT.Silu,
                                     bias=par_s[:, P_BZA:P_BZA + 1]).then_inc(silu_done, 1)
                act.wait_ge(gate_mm, 5 * h + 2)
                nc.scalar.activation(zs_b[64:128, h, :], bank[6 + (5 * h + 1) % 2][0:64, :HALF], ACT.Silu,
                                     bias=par_s[0:64, P_BZB:P_BZB + 1]).then_inc(silu_done, 1)

            project(0)
            high_w1(3)
            project(1)
            short_mid(0)
            silus(0)
            high_w1(4)
            evacuate(0, 3, tr_done, 3)
            high_w1(5)
            evacuate(0, 4, tr_done, 2)
            project(2)
            project(3)
            short_mid(1)
            high_w2(0)
            high_w2(1)
            silus(1)
            high_w2(2)
            high_w2(3)
            evacuate(1, 0, tr2_done, 4)
            evacuate(1, 1, tr2_done, 4)
            high_w2(4)
            high_w2(5)

            def gelu(i):
                c, j = steps[i]
                w = chunk_cols(c)[1]
                act.wait_ge(up_done, i + 1)
                if i >= RING:
                    act.wait_ge(gm_done, i - RING + 1)
                nc.scalar.activation(ge[:, i % RING, :w], bank[6 + i % 2][:, :w], ACT.Gelu,
                                     bias=par_s[:, P_B1 + j:P_B1 + j + 1]).then_inc(gelu_done, 1)

            def high(i):
                w = chunk_cols(steps[i][0])[1]
                act.wait_ge(gm_done, i + 1)
                if i >= RING:
                    act.wait_ge(down_done, i - RING + 1)
                nc.scalar.activation(gmh[:, i % RING, :w], gm[:, i % RING, :w], ACT.Copy).then_inc(gmh_done, 1)

            for i in range(NS + 1):
                if i < NS:
                    gelu(i)
                if i >= 1:
                    high(i - 1)
                if i in (LN2_STEP, LN2_STEP + 1, LN2_STEP + 2):
                    evacuate(1, 2 + i - LN2_STEP, tr2_done, 4)

        @block.vector
        def _(dve):
            v = nc.vector
            v.memset(idle[:, :], 0.0).then_inc(idle_set, 1)

            def filter_spectrum():
                dve.wait_ge(spec_mm, 1)
                v.tensor_copy(spec_s[:, :, :], bank[5][:PF, :2 * D].rearrange("p (a d) -> p a d", a=2)).then_inc(spec_ev, 1)

            def stats(n, t, src):
                rows = TT[t][1]
                v.bn_stats(st[n][:rows, t, :], src[:rows, t, :]).then_inc(stat[n], 1)
                dve.wait_ge(stat[n], t + 1)
                v.bn_aggr(mv[n][:rows, t, :], st[n][:rows, t, :]).then_inc(var_ready[n], 1)
                if n == 1:
                    dve.wait_ge(var_ready[1], 2 * t + 1)
                    v.tensor_scalar(mv[1][:rows, t, 1:2], mv[1][:rows, t, 1:2], EPS, None, ALU.add).then_inc(var_ready[1], 1)

            def embed(t):
                rows = TT[t][1]
                dve.wait_ge(tok_done, t + 1)
                v.tensor_tensor(h_s[:rows, t, :], bank[t % 2][:rows, :D], tokb_s[:rows, :], ALU.add).then_inc(h_ready, 1)
                dve.wait_ge(h_ready, t + 1)
                stats(0, t, h_s)

            def normalise(n, t, src):
                rows = TT[t][1]
                if n == 0:
                    dve.wait_ge(sd_ready[0], t + 1)
                    v.reciprocal(rs[n][:rows, t:t + 1], sd[n][:rows, t:t + 1]).then_inc(rs_ready[n], 1)
                dve.wait_ge(rs_ready[n], t + 1)
                v.tensor_scalar(xn[n][:rows, t, :DA], src[:rows, t, :DA], mv[n][:rows, t, 0:1], rs[n][:rows, t:t + 1],
                                ALU.subtract, ALU.mult).then_inc(xn_ready[n], 1)
                v.tensor_scalar(xn[n][:rows, t, DA:].rearrange("p (a d) -> p a d", a=2),
                                src[:rows, t:t + 1, DA:].broadcast_to([rows, 2, DB]), mv[n][:rows, t, 0:1],
                                rs[n][:rows, t:t + 1], ALU.subtract, ALU.mult).then_inc(xn_ready[n], 1)

            def cut(n, t):
                s, rows = TT[t]
                c = slice(s, s + rows)
                dve.wait_ge(xt_ready[n], t + 1)
                v.tensor_copy(xth[n][:, :, c], xt32[n][:, :, c]).then_inc(hi_ready[n], 1)
                dve.wait_ge(hi_ready[n], t + 1)
                v.tensor_tensor(xtl[n][:, c], xt32[n][:, 0, c], xth[n][:, 0, c].bitcast(f32), ALU.subtract).then_inc(split[n], 1)
                v.tensor_tensor(xth[n][64:128, 1, c], xt32[n][64:128, 1, c], xth[n][64:128, 1, c].bitcast(f32),
                                ALU.subtract).then_inc(split[n], 1)

            def spectrum(p):
                dve.wait_ge(fwd_done, p + 1)
                dve.wait_ge(spec_ev, 1)
                for k in range(2):
                    v.tensor_tensor(p_s[k][:, 2 * p:2 * p + 2, :], bank[5][:PF, :2 * D].rearrange("p (a d) -> p a d", a=2),
                                    spec_s[:, k:k + 1, :].broadcast_to([PF, 2, D]), ALU.mult).then_inc(spec_mul, 1)

            def short(h):
                im = slice(h * HIM, (h + 1) * HIM)
                for k, (xs, x, w) in enumerate(((xs_a, xt32[0][:, 0, :], P_WSA), (xs_b, xt32[0][0:DB, 1, :], P_WSB))):
                    rows = (DA, DB)[k]
                    xv = x.rearrange("p (b l) -> p b l", l=SEQ)[:, im, :]
                    sv = xs[:, :].rearrange("p (b l) -> p b l", l=SEQ)[:, im, :]
                    dve.wait_ge(xs_mid, 2 * h + k + 1)
                    v.scalar_tensor_tensor(sv[:, :, 1:], xv[:, :, :-1], par_s[0:rows, w:w + 1], sv[:, :, 1:],
                                           ALU.mult, ALU.add).then_inc(xs_step, 1)
                for k, (xs, x, w) in enumerate(((xs_a, xt32[0][:, 0, :], P_WSA), (xs_b, xt32[0][0:DB, 1, :], P_WSB))):
                    rows = (DA, DB)[k]
                    xv = x.rearrange("p (b l) -> p b l", l=SEQ)[:, im, :]
                    sv = xs[:, :].rearrange("p (b l) -> p b l", l=SEQ)[:, im, :]
                    dve.wait_ge(xs_step, 4 * h + k + 1)
                    v.scalar_tensor_tensor(sv[:, :, :-1], xv[:, :, 1:], par_s[0:rows, w + 2:w + 3], sv[:, :, :-1],
                                           ALU.mult, ALU.add).then_inc(xs_step, 1)

            def gates(h):
                b = [bank[6 + (5 * h + m) % 2] for m in range(5)]
                dve.wait_ge(silu_done, 2 * h + 2)
                v.scalar_tensor_tensor(u_b[:, h, :], b[1][64:128, :HALF], par_s[64:128, P_BZB:P_BZB + 1],
                                       zs_b[64:128, h, :], ALU.add, ALU.mult).then_inc(gate_done, 1)
                dve.wait_ge(gate_mm, 5 * h + 3)
                v.scalar_tensor_tensor(u_a[:, h, :], b[2][:, :HALF], par_s[:, P_BV1A:P_BV1A + 1],
                                       zs_a[:, h, :], ALU.add, ALU.mult).then_inc(gate_done, 1)
                dve.wait_ge(gate_mm, 5 * h + 4)
                dve.wait_ge(gate_done, 4 * h + 2)
                v.scalar_tensor_tensor(g_a[:, h, :], b[3][:, :HALF], par_s[:, P_BV2A:P_BV2A + 1],
                                       u_a[:, h, :], ALU.add, ALU.mult).then_inc(gate_done, 1)
                dve.wait_ge(gate_mm, 5 * h + 5)
                v.scalar_tensor_tensor(g_b[:, h, :], b[4][0:DB, :HALF], par_s[0:DB, P_BV2B:P_BV2B + 1],
                                       u_b[:, h, :], ALU.add, ALU.mult).then_inc(gate_done, 1)

            def mix(h):
                c = slice(h * HALF, (h + 1) * HALF)
                dve.wait_ge(gate_done, 4 * h + 4)
                dve.wait_ge(xs_step, 4 * h + 4)
                for k, (y, g, r) in enumerate(((y_a, g_a, DA), (y_b, g_b, DB))):
                    dve.wait_ge(inv_done, 2 * h + k + 1)
                    v.tensor_tensor(y[:, c], bank[k][:r, :HALF], g[:, h, :], ALU.mult).then_inc(y_done, 1)
                for k, (yt, y, xs) in enumerate(((yt_a, y_a, xs_a), (yt_b, y_b, xs_b))):
                    dve.wait_ge(y_done, 2 * h + k + 1)
                    v.tensor_tensor(yt[:, c], y[:, c], xs[:, c], ALU.add).then_inc(yt_done, 1)

            def residual(t):
                rows = TT[t][1]
                dve.wait_ge(wo_done, t + 1)
                dve.wait_ge(hb_ready, t + 1)
                v.tensor_tensor(h2_s[:rows, t, :], bank[2 + t % 2][:rows, :D], hb_s[:rows, t, :], ALU.add).then_inc(h2_ready, 1)
                dve.wait_ge(h2_ready, t + 1)
                stats(1, t, h2_s)

            def logits(c):
                ts = CHUNKS[c]
                n, w = len(ts), slice(ts[0], ts[-1] + 1)
                dve.wait_ge(lg_set, 1)
                dve.wait_ge(rt_done, c + 1)
                for t in ts:
                    rows = TT[t][1]
                    v.tensor_tensor(lg[:rows, t, :], bank[5][:rows, t * E:(t + 1) * E], rb_s[:rows, :], ALU.add).then_inc(lg_ev, 1)
                for t in ts:
                    dve.wait_ge(lg_ev, t + 1)
                    v.max(mx[:, t, :], lg[:, t, :]).then_inc(mx_ready, 1)
                dve.wait_ge(mx_ready, ts[-1] + 1)
                v.tensor_tensor(dl[:, w, :], lg[:, w, :], mx[:, w, 0:1].broadcast_to([128, n, E]), ALU.subtract).then_inc(dl_ready, 1)
                for t in ts:
                    last = v.max_index(ix[:, t, :], mx[:, t, :], lg[:, t, :])
                last.then_inc(ix_ready, 1)
                dve.wait_ge(ix_ready, 2 * c + 1)
                v.tensor_copy(ixf[:, w, :], ix[:, w, 0:2]).then_inc(ix_ready, 1)
                dve.wait_ge(ix_ready, 2 * c + 2)
                iota = iota_s[:, None, :].broadcast_to([128, n, E])
                v.tensor_tensor(m1[:, w, :], iota, ixf[:, w, 0:1].broadcast_to([128, n, E]), ALU.is_equal).then_inc(best, 1)
                v.tensor_tensor(m2[:, w, :], iota, ixf[:, w, 1:2].broadcast_to([128, n, E]), ALU.is_equal).then_inc(best, 1)
                dve.wait_ge(best, 4 * c + 2)
                v.tensor_tensor(mk[:, w, :], m1[:, w, :], m2[:, w, :], ALU.add).then_inc(best, 1)

            def gate_values(c):
                ts = CHUNKS[c]
                n, w = len(ts), slice(ts[0], ts[-1] + 1)
                dve.wait_ge(exp_done, c + 1)
                v.reduce_sum(se[:, w], ex[:, w, :], axis=AX.X).then_inc(sum_ready, 1)
                dve.wait_ge(best, 4 * c + 3)
                v.tensor_tensor(em[:, w, :], ex[:, w, :], mk[:, w, :], ALU.mult).then_inc(best, 1)
                dve.wait_ge(sum_ready, 2 * c + 1)
                v.reciprocal(re[:, w], se[:, w]).then_inc(sum_ready, 1)
                dve.wait_ge(best, 4 * c + 4)
                dve.wait_ge(sum_ready, 2 * c + 2)
                v.tensor_tensor(gt[:, w, :], em[:, w, :], re[:, w, None].broadcast_to([128, n, E]), ALU.mult).then_inc(ghl_ready, 1)
                dve.wait_ge(ghl_ready, 3 * c + 1)
                v.tensor_copy(ghl[:, w, 0:E].bitcast(f32r), gt[:, w, :]).then_inc(ghl_ready, 1)
                dve.wait_ge(ghl_ready, 3 * c + 2)
                v.tensor_tensor(ghl[:, w, E:2 * E], gt[:, w, :], ghl[:, w, 0:E], ALU.subtract).then_inc(ghl_ready, 1)

            def gates_down(c):
                s, cols = chunk_cols(c)
                dve.wait_ge(gtr_done, c + 1)
                v.tensor_copy(gT[:, s:s + cols], bank[5][:2 * E, :cols]).then_inc(gT_ready, 1)

            def weigh(i):
                w = chunk_cols(steps[i][0])[1]
                dve.wait_ge(gelu_done, i + 1)
                dve.wait_ge(gb_done, i + 1)
                v.tensor_tensor(gm[:, i % RING, :w], bank[i % 2][:, :w], ge[:, i % RING, :w], ALU.mult).then_inc(gm_done, 1)

            def low(i):
                w = chunk_cols(steps[i][0])[1]
                dve.wait_ge(gmh_done, i + 1)
                v.tensor_tensor(gml[:, i % RING, :w], gm[:, i % RING, :w], gmh[:, i % RING, :w].bitcast(f32),
                                ALU.subtract).then_inc(gml_done, 1)

            def finish(c):
                for k, t in enumerate(CHUNKS[c]):
                    rows = TT[t][1]
                    if k < len(CHUNKS[c]) - 1:
                        dve.wait_ge(acc_done, t + 1 - c)
                    else:
                        dve.wait_ge(down_done, (c + 1) * HC)
                    v.tensor_tensor(o_s[:rows, t, :], bank[2 + k][:rows, :D], h2_s[:rows, t, :], ALU.add).then_inc(fin_done, 1)

            dve.wait_ge(ld_128, 16)
            embed(0)
            dve.wait_ge(win_hi, 1)
            v.tensor_tensor(win_l[:, 0, :], win_s[:, 0, :], win_h[:, 0, :].bitcast(f32), ALU.subtract).then_inc(win_lo, 1)
            normalise(0, 0, h_s)
            embed(1)
            dve.wait_ge(win_hi, 2)
            v.tensor_tensor(win_l[:, 1, :], win_s[:, 1, :], win_h[:, 1, :].bitcast(f32), ALU.subtract).then_inc(win_lo, 1)
            normalise(0, 1, h_s)
            embed(2)
            cut(0, 0)
            normalise(0, 2, h_s)
            cut(0, 1)
            embed(3)
            cut(0, 2)
            normalise(0, 3, h_s)
            filter_spectrum()
            embed(4)
            spectrum(0)
            normalise(0, 4, h_s)
            gates(0)
            spectrum(1)
            cut(0, 3)
            cut(0, 4)
            short(0)
            mix(0)
            spectrum(2)
            residual(0)
            residual(1)
            spectrum(3)
            gates(1)
            normalise(1, 0, h2_s)
            normalise(1, 1, h2_s)
            short(1)
            cut(1, 0)
            cut(1, 1)
            mix(1)
            logits(0)
            residual(2)
            residual(3)
            gate_values(0)
            residual(4)
            gates_down(0)
            for i in range(NS + 1):
                if i < NS:
                    weigh(i)
                if i >= 1:
                    low(i - 1)
                if i in (0, 1, 2):
                    normalise(1, 2 + i, h2_s)
                if i in (LN2_STEP, LN2_STEP + 1, LN2_STEP + 2):
                    cut(1, 2 + i - LN2_STEP)
                if i == LN2_STEP + 4:
                    logits(1)
                if i == LN2_STEP + 6:
                    gate_values(1)
                if i == LN2_STEP + 8:
                    gates_down(1)
                if i == HC + DOWN_LAG - G_LAG - 1:
                    finish(0)
            finish(1)

        @block.tensor
        def _(pe):
            mm = nc.tensor.matmul

            def five(dst, rows, cols, n, w_h, w_l, x_side, start=True, stop=True):
                terms = ((xth[n][:, 0], w_h[:, 0]), (xth[n][:, 0], w_l[:, 0]), (xtl[n], w_h[:, 0]),
                         (xth[n][:, 1], w_h[:, 1]), (xth[n][:, 1], w_l[:, 1]))
                for k, (x, w) in enumerate(terms):
                    a, b = x[:, rows], w[:, cols]
                    if x_side == "moving":
                        a, b = b, a
                    last = mm(dst, a, b, start=start and k == 0, stop=stop and k == len(terms) - 1)
                return last

            pe.wait_ge(idle_set, 1)
            for _ in range(WARM):
                mm(bank[7][:, :], idle[:, :128], idle[:, :], start=True, stop=True)

            def filter_spectrum():
                pe.wait_ge(ld_65, 16)
                for k in range(2):
                    last = mm(bank[5][:PF, k * D:(k + 1) * D], basis_s[:, k, :], waug_s, start=True, stop=True)
                last.then_inc(spec_mm, 1)

            def embed(t):
                s, n = TT[t]
                pe.wait_ge(ld_x[t], 16)
                if t >= 2:
                    pe.wait_ge(h_ready, t - 1)
                for k in range(KP):
                    last = mm(bank[t % 2][:n, :D], x_s[:, KP * s + k * n:KP * s + (k + 1) * n], tokw_s[:, k, :],
                              start=k == 0, stop=k == KP - 1)
                last.then_inc(tok_done, 1)

            def transpose(n, t, b, done):
                rows = TT[t][1]
                pe.wait_ge(xn_ready[n], 2 * t + 2)
                if t >= 2 - n:
                    pe.wait_ge(xt_ready[n], t - 1 + n)
                nc.tensor.transpose(bank[b][:, 0:rows], xn[n][:rows, t, 0:DA], ident_s[:rows, :rows])
                nc.tensor.transpose(bank[b][:, 128:128 + rows], xn[n][:rows, t, DA:], ident_s[:rows, :rows]).then_inc(done, 1)

            def project(p):
                pe.wait_ge(split[0], 2 * (tile_of((2 * p + 2) * PTOK - 1) + 1))
                if p == 0:
                    pe.wait_ge(win_lo, 2)
                else:
                    pe.wait_ge(px_ev, p)
                for q in range(2):
                    g = 2 * p + q
                    last = five(bank[4][:PTOK, q * D:(q + 1) * D], slice(g * PTOK, (g + 1) * PTOK), slice(0, D), 0,
                                win_h, win_l, "stationary")
                last.then_inc(px_done, 1)

            def forward(p):
                pe.wait_ge(px_ev, p + 1)
                if p == 0:
                    pe.wait_ge(ld_binx, 16)
                    pe.wait_ge(ld_108, 16)
                    pe.wait_ge(spec_ev, 1)
                else:
                    pe.wait_ge(spec_mul, 2 * p)
                mm(bank[5][:PF, :2 * D], fwd_s, xp_s[:, 2 * p:2 * p + 2, :], start=True, stop=True).then_inc(fwd_done, 1)

            def gate(h, m):
                i = 5 * h + m
                if i >= 2:
                    j = i - 2
                    if j % 5 == 0:
                        pe.wait_ge(silu_done, 2 * (j // 5) + 1)
                    else:
                        pe.wait_ge(gate_done, 4 * (j // 5) + j % 5)
                c0, w = GATE_COL[m]
                five(bank[6 + i % 2][:w, :HALF], slice(h * HALF, (h + 1) * HALF), slice(c0, c0 + w), 0,
                     win_h, win_l, "moving").then_inc(gate_mm, 1)

            def inverse(h):
                pe.wait_ge(spec_mul, 4 * (h + 1))
                if h == 0:
                    pe.wait_ge(h_ready, NT)
                else:
                    pe.wait_ge(y_done, 2)
                for k, (d0, d1) in enumerate(((0, DA), (DA, D))):
                    for g in range(PAIRS // 2):
                        for part in range(2):
                            last = mm(bank[k][:d1 - d0, g * PTOK:(g + 1) * PTOK], p_s[part][:, h * PAIRS // 2 + g, d0:d1],
                                      inv_s[:, part, :], start=part == 0, stop=part == 1)
                    last.then_inc(inv_done, 1)

            def merge(t):
                s, n = TT[t]
                pe.wait_ge(yt_done, 2 * ((s + n - 1) // HALF + 1))
                if t < 2:
                    pe.wait_ge(xt_ready[0], NT)
                    pe.wait_ge(ld_late, 16)
                else:
                    pe.wait_ge(h2_ready, t - 1)
                b = bank[2 + t % 2][:n, :D]
                mm(b, yt_a[:, s:s + n], woa_s, start=True, stop=False)
                mm(b, yt_b[:, s:s + n], wob_s, start=False, stop=True).then_inc(wo_done, 1)

            def logits(c):
                if c == 0:
                    pe.wait_ge(sm_lo, 2)
                    pe.wait_ge(spec_mul, 8)
                else:
                    pe.wait_ge(gT_ready, 1)
                for t in CHUNKS[c]:
                    s, n = TT[t]
                    pe.wait_ge(split[1], 2 * (t + 1))
                    last = five(bank[5][:n, t * E:(t + 1) * E], slice(s, s + n), slice(0, E), 1, rw_h, rw_l, "stationary")
                last.then_inc(rt_done, 1)

            def gates_across(c):
                pe.wait_ge(ghl_ready, 3 * c + 3)
                s0 = chunk_cols(c)[0]
                for t in CHUNKS[c]:
                    s, n = TT[t]
                    last = nc.tensor.transpose(bank[5][:2 * E, s - s0:s - s0 + n], ghl[:n, t, :], ident_s[:n, :n])
                last.then_inc(gtr_done, 1)

            def up(i):
                c, j = steps[i]
                s, w = chunk_cols(c)
                if i == 0:
                    pe.wait_ge(gate_done, 8)
                if i >= 2:
                    pe.wait_ge(gelu_done, i - 1)
                if c == 0 and j % 3 == 0:
                    pe.wait_ge(w1_lo, j // 3 + 1)
                five(bank[6 + i % 2][:, :w], slice(s, s + w), slice(j * 128, (j + 1) * 128), 1, w1_h, w1_l,
                     "moving").then_inc(up_done, 1)

            def spread(i):
                c, j = steps[i]
                s, w = chunk_cols(c)
                if i == 0:
                    pe.wait_ge(ld_sel, 16)
                    pe.wait_ge(y_done, 4)
                if j == 0:
                    pe.wait_ge(gT_ready, c + 1)
                if i >= 2:
                    pe.wait_ge(gm_done, i - 1)
                mm(bank[i % 2][:, :w], sel_r[:, j * 128:(j + 1) * 128], gT[:, s:s + w], start=True,
                   stop=True).then_inc(gb_done, 1)

            def down(i):
                c, j = steps[i]
                s0 = chunk_cols(c)[0]
                pe.wait_ge(gmh_done, i + 1)
                pe.wait_ge(gml_done, i + 1)
                if c == 0 and j % 3 == 0:
                    pe.wait_ge(w2_lo, j // 3 + 1)
                if j == 0:
                    if c == 0:
                        pe.wait_ge(h2_ready, NT)
                    else:
                        pe.wait_ge(fin_done, len(CHUNKS[0]))
                r = i % RING
                for k, t in enumerate(CHUNKS[c]):
                    s, n = TT[t]
                    acc = bank[2 + k][:n, :D]
                    rows = slice(s - s0, s - s0 + n)
                    if j == 0:
                        mm(acc, gT[:, s:s + n], b2_h[:, :], start=True, stop=False)
                        mm(acc, gT[:, s:s + n], b2_l[:, :], start=False, stop=False)
                    mm(acc, gmh[:, r, rows], w2_h[:, j, :], start=False, stop=False)
                    mm(acc, gmh[:, r, rows], w2_l[:, j, :], start=False, stop=False)
                    last = mm(acc, gml[:, r, rows], w2_h[:, j, :], start=False, stop=j == HC - 1)
                    if j == HC - 1 and k < len(CHUNKS[c]) - 1:
                        last.then_inc(acc_done, 1)
                last.then_inc(down_done, 1)

            pe.wait_ge(ld_tokw, 16)
            embed(0)
            embed(1)
            embed(2)
            pe.wait_ge(ld_128, 16)
            transpose(0, 0, 2, tr_done)
            embed(3)
            transpose(0, 1, 3, tr_done)
            filter_spectrum()
            transpose(0, 2, 2, tr_done)
            project(0)
            embed(4)
            project(1)
            gate(0, 0)
            forward(0)
            gate(0, 1)
            gate(0, 2)
            forward(1)
            gate(0, 3)
            gate(0, 4)
            transpose(0, 3, 3, tr_done)
            transpose(0, 4, 2, tr_done)
            inverse(0)
            project(2)
            project(3)
            gate(1, 0)
            forward(2)
            gate(1, 1)
            merge(0)
            merge(1)
            forward(3)
            gate(1, 2)
            gate(1, 3)
            gate(1, 4)
            inverse(1)
            transpose(1, 0, 4, tr2_done)
            transpose(1, 1, 4, tr2_done)
            logits(0)
            for i in range(NS + DOWN_LAG):
                if i == 1:
                    merge(2)
                    merge(3)
                    merge(4)
                    gates_across(0)
                if i < NS:
                    up(i)
                if 0 <= i - G_LAG < NS:
                    spread(i - G_LAG)
                if i >= DOWN_LAG:
                    down(i - DOWN_LAG)
                if i in (LN2_STEP - 1, LN2_STEP, LN2_STEP + 1):
                    transpose(1, 3 + i - LN2_STEP, 4, tr2_done)
                if i == LN2_STEP + 3:
                    logits(1)
                if i == LN2_STEP + 7:
                    gates_across(1)


def constants():
    import numpy as np
    k = np.arange(SEQ)
    f_cos, f_sin = np.arange(POINTS // 2 + 1), np.arange(1, POINTS // 2)
    turn = 2 * np.pi / POINTS
    trig = np.concatenate([np.cos(turn * np.outer(f_cos, k)), np.sin(turn * np.outer(f_sin, k))])
    pos = np.sin(np.outer(k, np.arange(TAPS)) / TAPS)
    pos = np.concatenate([pos, np.ones((SEQ, 1))], 1)
    f_all = np.concatenate([f_cos, f_sin])
    basis = np.stack([np.cos(turn * np.outer(f_all, k)) @ pos, np.sin(turn * np.outer(f_all, k)) @ pos])
    basis = np.concatenate([basis, basis], 1).transpose(2, 0, 1)
    fwd = np.zeros((PTOK + 1, PF))
    inv = np.zeros((PF, 2, PTOK))
    theta = turn * np.outer(f_all, k - SEQ // 2)
    weight = np.where((f_all == 0) | (f_all == POINTS // 2), 1.0, 2.0)[:, None] / POINTS
    is_cos = (np.arange(POINTS) < len(f_cos))[:, None]
    first = weight * np.where(is_cos, np.cos(theta), np.sin(theta))
    second = weight * np.where(is_cos, -np.sin(theta), np.cos(theta))
    for b in range(2):
        rows, cols = slice(b * SEQ, (b + 1) * SEQ), slice(b * POINTS, (b + 1) * POINTS)
        fwd[rows, cols] = trig.T
        inv[cols, 0, rows] = first
        inv[cols, 1, rows] = second
    fwd[PTOK] = fwd.sum(0)
    expert = np.arange(HC * 128) // HID
    sel = np.tile((np.arange(E)[:, None] == expert[None, :]), (2, 1))
    made = dict(basis=basis.reshape(TAPS + 1, -1), fwd=fwd, inv=inv.reshape(PF, -1), ident=np.eye(128),
                iota=np.tile(np.arange(E), (128, 1)), sel=sel)
    return {n: np.ascontiguousarray(a, dtype=np.float32) for n, a in made.items()}


def kernel(x, L0_tok_W, L0_tok_b, L0_attn_w_in, L0_attn_b_in, L0_attn_w_filt, L0_attn_b_filt,
           L0_attn_w_short, L0_attn_b_short, L0_attn_w_out, L0_attn_b_out, L0_ffn_router_w,
           L0_ffn_router_b, L0_ffn_w1, L0_ffn_b1, L0_ffn_w2, L0_ffn_b2):
    import numpy as np
    import concourse.bacc as bacc
    from concourse.bass_utils import run_bass_kernel_spmd

    def split_rows(w, twice):
        return w[:DA], np.concatenate([w[DA:], w[DA:]]) if twice else w[DA:]

    a = {k: np.asarray(v) for k, v in locals().items() if k == "x" or k.startswith("L0_")}
    patches = a["x"].reshape(IMAGES, 3, 6, 16, 6, 16).transpose(1, 3, 5, 0, 2, 4).reshape(KP, 128, TOK)
    xt = np.concatenate([patches[:, :, s:s + n].transpose(1, 0, 2).reshape(128, KP * n) for s, n in TT], 1)
    order = np.concatenate([np.arange(0, D), D + np.arange(DA), D + np.arange(DA, D), 2 * D + np.arange(DA, D),
                            2 * D + np.arange(DA), 3 * D + np.arange(DA), 3 * D + np.arange(DA, D)])
    win_a, win_b = split_rows(a["L0_attn_w_in"][:, order], True)
    b_in, w_short, b_short = a["L0_attn_b_in"], a["L0_attn_w_short"][:, 0, :], a["L0_attn_b_short"]
    par = np.zeros((128, NPAR), np.float32)
    par[:, P_BZA] = b_in[D:D + DA]
    par[:, P_BZB] = np.concatenate([b_in[D + DA:2 * D], b_in[2 * D + DA:3 * D]])
    par[:, P_BV1A] = b_in[2 * D:2 * D + DA]
    par[:, P_BV2A] = b_in[3 * D:3 * D + DA]
    par[:DB, P_BV2B] = b_in[3 * D + DA:]
    par[:, P_WSA:P_WSA + 3] = w_short[:DA]
    par[:DB, P_WSB:P_WSB + 3] = w_short[DA:]
    par[:, P_BSA] = b_short[:DA]
    par[:DB, P_BSB] = b_short[DA:]
    par[:, P_B1:] = a["L0_ffn_b1"].reshape(HC, 128).T
    wo_a, wo_b = split_rows(a["L0_attn_w_out"], False)
    rw_a, rw_b = split_rows(a["L0_ffn_router_w"], True)
    w1 = np.stack(split_rows(a["L0_ffn_w1"].transpose(1, 0, 2).reshape(D, HC * 128), True), 1)
    w1 = w1.reshape(128, 2, PIECES, W1P).transpose(0, 2, 1, 3).reshape(128, PIECES, 2 * W1P)
    const = constants()

    def pack(rows, layout, **parts):
        assert {n: p.shape[1] for n, p in parts.items()} == layout, (rows, layout)
        return np.concatenate([np.pad(p, ((0, rows - len(p)), (0, 0))) for p in parts.values()], 1)

    def all_rows(row):
        return np.tile(row, (128, 1))

    arrays = dict(
        xt=xt, tokw=a["L0_tok_W"].T.reshape(KP, 128, D).transpose(1, 0, 2), win=np.stack([win_a, win_b], 1), binx=b_in[:D],
        rows128=pack(128, ROWS128, ident=const["ident"], tokb=all_rows(a["L0_tok_b"]), par=par, iota=const["iota"],
                     rb=all_rows(a["L0_ffn_router_b"]), rw=np.concatenate([rw_a, rw_b], 1)),
        rows65=pack(TAPS + 1, ROWS65, waug=np.concatenate([a["L0_attn_w_filt"], a["L0_attn_b_filt"][None]]),
                    basis=const["basis"]),
        rows108=pack(PF, ROWS108, fwd=const["fwd"], inv=const["inv"]),
        late128=pack(128, LATE128, wo_a=wo_a, wo_b=wo_b, bout=all_rows(a["L0_attn_b_out"])),
        b2=np.concatenate([a["L0_ffn_b2"]] * 2), w1=w1,
        w2=a["L0_ffn_w2"].reshape(HC, 128, D).transpose(1, 0, 2).reshape(128, PIECES, W2P * D), c_sel=const["sel"])
    arrays = {k: np.ascontiguousarray(v) for k, v in arrays.items()}
    nc = bacc.Bacc("TRN2", target_bir_lowering=False, num_devices=1)
    args = [nc.dram_tensor(k, v.shape, mybir.dt.from_np(v.dtype), kind="ExternalInput").ap() for k, v in arrays.items()]
    out = nc.dram_tensor("out", (TOK, D), mybir.dt.float32, kind="ExternalOutput").ap()
    build(nc, *args, out)
    r = run_bass_kernel_spmd(nc, [arrays], core_ids=[0])
    return r.results[0]["out"].reshape(IMAGES, SEQ, D)
```

```python
import math

import concourse.bass as bass
from concourse import mybir
from contextlib import ExitStack

D = 192
DA, DB = 128, 64
IMAGES, SEQ = 16, 36
TOK = IMAGES * SEQ
TT = [(s, min(128, TOK - s)) for s in range(0, TOK, 128)]
NT = len(TT)
PIX = 768
KP = PIX // 128
PAIRS = IMAGES // 2
PTOK = 2 * SEQ
POINTS = 54
PF = 2 * POINTS
HALF = TOK // 2
HIM = IMAGES // 2
TAPS = 64
E = 8
HID = 288
HC = E * HID // 128
SPREAD_TILES = [(2 * e, 2 * e + 1) for e in range(E)] + [(j,) for j in range(2 * E, HC)]
GATE_COL = [(192, 128), (320, 128), (448, 128), (576, 128), (704, 64)]
P_BZA, P_BZB, P_BV1A, P_BV2A, P_BV2B, P_WSA, P_WSB, P_BSA, P_BSB, P_B1 = 0, 1, 2, 3, 4, 5, 8, 11, 12, 13
NPAR = P_B1 + HC
CHUNKS = [(0, 1), (2, 3, 4)]
EPS = 1e-5
W2_STEPS = {0: 1, 1: 2, 3: 3, 5: 4, 11: 5}
LN2_STEPS = {1: 2, 2: 3, 4: 4}
ROUTE_STEP = 10
PIECES = 6
W1P = HC * 128 // PIECES
W2P = HC // PIECES
WARM = 9
GE_RING, RING = 5, 6
FOLD = [(HC - 2, HC - 1), (HC - 7, HC - 6, HC - 3)]
ACC_BANK = [(2, 3, 3, 5, 4), (4, 2, 2, 3, 5)]
TR2_BANK = (4, 2, 4, 5, 4)
MERGE_BANK = (2, 3, 2, 3, 4)
TR2_LAG = 5
HIGH_LAG, DOWN_LAG = 2, 5

ROWS128 = dict(ident=128, tokb=D, par=NPAR, iota=E, rb=E, rw=2 * E)
ROWS65 = dict(waug=D, basis=2 * PF)
ROWS108 = dict(fwd=PF, inv=2 * PTOK)
LATE128 = dict(wo_a=D, wo_b=D, bout=D)


def columns(pack):
    at, found = 0, {}
    for name, width in pack.items():
        found[name] = slice(at, at + width)
        at += width
    return found


def build(nc, xt, tokw, win, binx, rows128, rows65, rows108, late128, b2, w1, w2, c_sel, out):
    f32, f32r, u32 = mybir.dt.float32, mybir.dt.float32r, mybir.dt.uint32
    ALU, ACT, AX = mybir.AluOpType, mybir.ActivationFunctionType, mybir.AxisListType
    ctx = ExitStack()
    with ctx:
        def sb(name, shape, dt=f32):
            return ctx.enter_context(nc.sbuf_tensor(name, shape, dt))

        def sem(name):
            return ctx.enter_context(nc.semaphore(name))

        x_s = sb("x_s", [128, KP * TOK])
        tokw_s = sb("tokw_s", [128, KP, D])
        win_s = sb("win_s", [128, 2, 4 * D])
        win_h = sb("win_h", [128, 2, 4 * D], f32r)
        win_l = sb("win_l", [128, 2, 4 * D], f32r)
        pk128 = sb("pk128", [128, sum(ROWS128.values())])
        pk65 = sb("pk65", [TAPS + 1, sum(ROWS65.values())])
        pk108 = sb("pk108", [PF, sum(ROWS108.values())])
        pkl = sb("pkl", [128, sum(LATE128.values())])
        at = columns(ROWS128)
        ident_s, tokb_s, par_s, iota_s, rb_s = (pk128[:, at[n]] for n in ("ident", "tokb", "par", "iota", "rb"))
        rw_s = pk128[:, at["rw"]].rearrange("p (a e) -> p a e", a=2)
        at = columns(ROWS65)
        waug_s = pk65[:, at["waug"]]
        basis_s = pk65[:, at["basis"]].rearrange("p (a r) -> p a r", a=2)
        at = columns(ROWS108)
        fwd_s = pk108[:PTOK + 1, at["fwd"]]
        inv_s = pk108[:, at["inv"]].rearrange("p (a t) -> p a t", a=2)
        at = columns(LATE128)
        woa_s, wob_s, bout_s = pkl[:, at["wo_a"]], pkl[:DB, at["wo_b"]], pkl[:, at["bout"]]
        rw_hl = sb("rw_hl", [128, 2, 2, E], f32r)
        stage = sb("stage", [128, PIECES, 2 * W1P])
        w1_h = sb("w1_h", [128, 2, HC * 128], f32r)
        w1_l = sb("w1_l", [128, 2, HC * 128], f32r)
        w2_hl = sb("w2_hl", [128, HC, 2, D], f32r)
        b2_s = sb("b2_s", [2 * E, D])
        b2_hl = sb("b2_hl", [2 * E, 2, D], f32r)
        sel_r = sb("sel_r", [2 * E, len(SPREAD_TILES) * 128], f32r)
        eps_s = sb("eps_s", [128, 1])
        scrap = sb("scrap", [128, 4])
        minus_half = sb("minus_half", [128, 1])
        euler = sb("euler", [128, E * len(CHUNKS[-1])])
        idle = sb("idle", [128, 512], mybir.dt.bfloat16)
        h_s = sb("h_s", [128, NT, D])
        hb_s = sb("hb_s", [128, NT, D])
        h2_s = sb("h2_s", [128, NT, D])
        o_s = h_s
        st = [sb(f"st{n}", [128, NT, 6]) for n in range(2)]
        mv = [sb(f"mv{n}", [128, NT, 2]) for n in range(2)]
        sd = [sb(f"sd{n}", [128, NT]) for n in range(2)]
        rs = [sb(f"rs{n}", [128, NT]) for n in range(2)]
        xn = sb("xn", [128, NT, 2 * DA])
        xt32 = sb("xt32", [128, 2, TOK])
        xth = sb("xth", [128, 2, TOK], f32r)
        xtl = sb("xtl", [128, TOK], f32r)
        spec_s = sb("spec_s", [PF, 2, D])
        xp_s = win_s[:PTOK + 1, :, :].rearrange("p a n -> p (a n)").rearrange("p (g d) -> p g d", d=D)
        p_s = [x_s[:PF, n * PAIRS * D:(n + 1) * PAIRS * D].rearrange("p (g d) -> p g d", d=D) for n in range(2)]
        zs_a = sb("zs_a", [DA, 2, HALF])
        zs_b = sb("zs_b", [128, 2, HALF])
        u_a = g_a = zs_a
        u_b = sb("u_b", [DB, 2, HALF])
        g_b = u_b
        xs_a = sb("xs_a", [DA, TOK])
        xs_b = sb("xs_b", [DB, TOK])
        yt_a = y_a = sb("y_a", [DA, TOK])
        yt_b = y_b = sb("y_b", [DB, TOK])
        tokw_flat = tokw_s[:, :, :].rearrange("p a d -> p (a d)")
        outer = [[tokw_flat[:(DA, DB)[k], (2 * k + tap) * HALF:(2 * k + tap + 1) * HALF] for tap in range(2)] for k in range(2)]
        lg = sb("lg", [128, NT, E])
        mx = sb("mx", [128, NT, E])
        ix = sb("ix", [128, NT, E], u32)
        ixf = sb("ixf", [128, NT, 2])
        dl = sb("dl", [128, NT, E])
        ex = sb("ex", [128, NT, E])
        m1 = sb("m1", [128, NT, E])
        m2 = sb("m2", [128, NT, E])
        mk = sb("mk", [128, NT, E])
        em = sb("em", [128, NT, E])
        se = sb("se", [128, NT])
        re = sb("re", [128, NT])
        gt = sb("gt", [128, NT, E])
        ghl = sb("ghl", [128, NT, 2 * E])
        gT = sb("gT", [2 * E, NT * 128], f32r)
        CW = max(sum(TT[t][1] for t in ts) for ts in CHUNKS)
        ge, gm = (x_s[:, n * GE_RING * CW:(n + 1) * GE_RING * CW].rearrange("p (r c) -> p r c", c=CW) for n in range(2))
        gmhl = sb("gmhl", [128, RING, 2 * CW], f32r)

        bank = [ctx.enter_context(nc.psum_tensor(f"bank{i}", [128, 512], f32)) for i in range(8)]

        ld_tokw, ld_win, ld_128, ld_65, ld_108, ld_late, ld_b2, ld_binx, ld_sel, stored = map(
            sem, ["ld_tokw", "ld_win", "ld_128", "ld_65", "ld_108", "ld_late", "ld_b2", "ld_binx", "ld_sel", "stored"])
        ld_w1, ld_w2 = ([sem(f"ld_{n}_{q}") for q in range(PIECES)] for n in ("w1", "w2"))
        ld_x0_rest, ld_tokw_rest = sem("ld_x0_rest"), sem("ld_tokw_rest")
        ld_x = [sem(f"ld_x{t}") for t in range(NT)]
        tok_done, spec_mm, tr_done, px_done, fwd_done, gate_mm, wo_done = map(
            sem, ["tok_done", "spec_mm", "tr_done", "px_done", "fwd_done", "gate_mm", "wo_done"])
        tr2_done, rt_done, gtr_done, up_done, gb_done, down_done, acc_done = map(
            sem, ["tr2_done", "rt_done", "gtr_done", "up_done", "gb_done", "down_done", "acc_done"])
        win_hi, w1_hi, w2_hi, sm_hi, win_lo, w1_lo, w2_lo, sm_lo = map(
            sem, ["win_hi", "w1_hi", "w2_hi", "sm_hi", "win_lo", "w1_lo", "w2_lo", "sm_lo"])
        idle_set, powers_set, no_gates_set = sem("idle_set"), sem("powers_set"), sem("no_gates_set")
        eps_set, lg_set, spec_ev, h_ready, hb_ready, h2_ready = map(
            sem, ["eps_set", "lg_set", "spec_ev", "h_ready", "hb_ready", "h2_ready"])
        xt_ready = sem("xt_ready")
        eps_added = [sem(f"eps_added{k}") for k in (1, 2)]
        stat, var_ready, sd_ready, rs_ready, xn_ready, hi_ready, split = (
            [sem(f"{n}{k}") for k in (1, 2)] for n in
            ("stat", "var_ready", "sd_ready", "rs_ready", "xn_ready", "hi_ready", "split"))
        px_ev, spec_mul, silu_done, gate_done, xs_mid, xs_step, yt_done = map(
            sem, ["px_ev", "spec_mul", "silu_done", "gate_done", "xs_mid", "xs_step", "yt_done"])
        inv_done, y_done = ([sem(f"{n}_{k}") for k in "ab"] for n in ("inv_done", "y_done"))
        lg_ev = [sem("lg_ev_0"), sem("lg_ev_1")]
        folded = sem("folded")
        mx_ready, dl_ready, ix_ready, best, exp_done, sum_ready, ghl_ready, gT_ready = map(
            sem, ["mx_ready", "dl_ready", "ix_ready", "best", "exp_done", "sum_ready", "ghl_ready", "gT_ready"])
        gelu_done, gm_done, gmh_done, gml_done, fin_done = map(
            sem, ["gelu_done", "gm_done", "gmh_done", "gml_done", "fin_done"])

        assert max(FOLD[-1]) <= HC - DOWN_LAG + 2
        steps = [(c, j) for c in range(len(CHUNKS)) for j in range(HC)]
        NS = len(steps)
        spreads = [(c, q) for c in range(len(CHUNKS)) for q in range(len(SPREAD_TILES))]

        def spread_of(i):
            c, j = steps[i]
            return c * len(SPREAD_TILES) + next(q for q, tiles in enumerate(SPREAD_TILES) if j in tiles)

        def chunk_cols(c):
            s = TT[CHUNKS[c][0]][0]
            return s, sum(TT[t][1] for t in CHUNKS[c])

        def piece1(q):
            return stage[:, q, :].rearrange("p (a n) -> p a n", a=2)

        def piece2(q):
            return stage[:, q, :W2P * D].rearrange("p (j d) -> p j d", d=D)

        def transposed(b, rows):
            return bank[b][:, :256].rearrange("p (a c) -> p a c", a=2)[:, :, :rows]

        def stacks(t):
            return 2 * TT[t][1] <= 128

        def high_cols(c, t):
            s, n = TT[t]
            at = s - chunk_cols(c)[0]
            return slice(at, at + n)

        def low_cols(c, t):
            w, last = chunk_cols(c)[1], CHUNKS[c][-1]
            if not stacks(last):
                shift = w
            elif t == last:
                shift = TT[last][1]
            else:
                shift = w + TT[last][1]
            at = high_cols(c, t)
            return slice(at.start + shift, at.stop + shift)

        def tile_of(token):
            return token // 128

        block = ctx.enter_context(nc.Block())

        @block.sync
        def _(sp):
            def load_x(t, halves=(0, 1)):
                s, n = TT[t]
                c = slice(KP * s + halves[0] * KP // 2 * n, KP * s + (halves[-1] + 1) * KP // 2 * n)
                done = ld_x0_rest if halves == (1,) else ld_x[t]
                sp.dma_start(x_s[:, c], xt[:, c]).then_inc(done, 16)

            load_x(0, (0,))
            load_x(0, (1,))
            load_x(1)
            load_x(2)
            sp.dma_start(win_s[:, :, :], win).then_inc(ld_win, 16)
            load_x(3)
            load_x(4)
            for q in range(PIECES):
                sp.dma_start(stage[:, q, :], w1[:, q, :]).then_inc(ld_w1[q], 16)
            sp.wait_ge(win_lo, 2)
            sp.dma_start(xp_s[PTOK:PTOK + 1, :, :], binx.partition_broadcast(PAIRS).rearrange("(o g) d -> o g d", o=1)).then_inc(ld_binx, 16)
            for q in range(PIECES):
                sp.wait_ge(w1_lo, q + 1)
                sp.dma_start(stage[:, q, :W2P * D], w2[:, q, :]).then_inc(ld_w2[q], 16)
            for t, (s, n) in enumerate(TT):
                sp.wait_ge(fin_done, t + 1)
                sp.dma_start(out[s:s + n, :], o_s[:n, t, :]).then_inc(stored, 16)
            sp.wait_ge(stored, 16 * NT)

        @block.gpsimd
        def _(pool):
            g = nc.gpsimd
            g.memset(eps_s[:, :], EPS).then_inc(eps_set, 1)
            g.memset(lg[:, :, :], 0.0).then_inc(lg_set, 1)
            g.memset(gT[:, TOK:].bitcast(f32), 0.0).then_inc(no_gates_set, 1)
            g.memset(minus_half[:, :], -0.5)
            g.memset(euler[:, :], math.e).then_inc(powers_set, 1)

            def low_w1(q):
                pool.wait_ge(w1_hi, q + 1)
                c = slice(q * W1P, (q + 1) * W1P)
                g.tensor_tensor(w1_l[:, :, c], piece1(q), w1_h[:, :, c].bitcast(f32), ALU.subtract).then_inc(w1_lo, 1)

            def low_w2(q):
                pool.wait_ge(w2_hi, q + 1)
                c = slice(q * W2P, (q + 1) * W2P)
                g.tensor_tensor(w2_hl[:, c, 1, :], piece2(q), w2_hl[:, c, 0, :].bitcast(f32), ALU.subtract).then_inc(w2_lo, 1)

            def with_bias(t):
                rows = TT[t][1]
                pool.wait_ge(h_ready, t + 1)
                g.tensor_tensor(hb_s[:rows, t, :], h_s[:rows, t, :], bout_s[:rows, :], ALU.add).then_inc(hb_ready, 1)

            for k in range(2):
                pool.wait_ge(win_hi, k + 1)
                g.tensor_tensor(win_l[:, k, :], win_s[:, k, :], win_h[:, k, :].bitcast(f32), ALU.subtract).then_inc(win_lo, 1)
            pool.wait_ge(sm_hi, 2)
            g.tensor_tensor(rw_hl[:, :, 1, :], rw_s, rw_hl[:, :, 0, :].bitcast(f32), ALU.subtract).then_inc(sm_lo, 1)
            g.tensor_tensor(b2_hl[:, 1, :], b2_s[:, :], b2_hl[:, 0, :].bitcast(f32), ALU.subtract).then_inc(sm_lo, 1)
            low_w1(0)

            def inverse_deviation(n, t):
                rows = TT[t][1]
                pool.wait_ge(var_ready[n], t + 1)
                g.tensor_scalar(mv[n][:rows, t, 1:2], mv[n][:rows, t, 1:2], EPS, None, ALU.add).then_inc(eps_added[n], 1)
                pool.wait_ge(eps_added[n], 1 if n == 0 else t + 1)
                g.tensor_tensor(rs[n][:rows, t:t + 1], mv[n][:rows, t, 1:2], minus_half[:rows, :], ALU.pow).then_inc(rs_ready[n], 1)

            def exponentials(c):
                ts = CHUNKS[c]
                w = slice(ts[0], ts[-1] + 1)
                pool.wait_ge(dl_ready, c + 1)
                powers_of = euler[:, :len(ts) * E].rearrange("p (t e) -> p t e", e=E)
                g.tensor_tensor(ex[:, w, :], powers_of, dl[:, w, :], ALU.pow).then_inc(exp_done, 1)

            def short(h):
                im = slice(h * HIM, (h + 1) * HIM)
                for tap in range(2):
                    for k, xs in enumerate((xs_a, xs_b)):
                        sv = xs[:, :].rearrange("p (b l) -> p b l", l=SEQ)[:, im, :]
                        ov = outer[k][tap].rearrange("p (b l) -> p b l", l=SEQ)
                        if tap == 0:
                            pool.wait_ge(xs_mid, 2 * h + k + 1)
                            dst, src = sv[:, :, 1:], ov[:, :, :-1]
                        else:
                            pool.wait_ge(xs_step, 4 * h + k + 1)
                            dst, src = sv[:, :, :-1], ov[:, :, 1:]
                        g.tensor_tensor(dst, dst, src, ALU.add).then_inc(xs_step, 1)

            pool.dma_start(sel_r[:, :], c_sel).then_inc(ld_sel, 16)
            pool.wait_ge(powers_set, 1)
            inverse_deviation(0, NT - 1)
            low_w1(1)
            pool.wait_ge(ld_late, 16)
            with_bias(0)
            with_bias(1)
            short(0)
            low_w1(2)
            low_w1(3)
            with_bias(2)
            with_bias(3)
            inverse_deviation(1, 0)
            inverse_deviation(1, 1)
            short(1)
            with_bias(4)
            low_w1(4)
            low_w1(5)
            low_w2(0)
            low_w2(1)
            low_w2(2)
            inverse_deviation(1, 2)
            inverse_deviation(1, 3)
            low_w2(3)
            inverse_deviation(1, 4)
            low_w2(4)
            low_w2(5)
            exponentials(1)

        @block.scalar
        def _(act):
            act.dma_start(tokw_s[:, :KP // 2, :], tokw[:, :KP // 2, :]).then_inc(ld_tokw, 16)
            act.dma_start(tokw_s[:, KP // 2:, :], tokw[:, KP // 2:, :]).then_inc(ld_tokw_rest, 16)
            act.dma_start(pk128[:, :], rows128).then_inc(ld_128, 16)
            act.dma_start(pk65[:, :], rows65).then_inc(ld_65, 16)
            act.dma_start(pk108[:, :], rows108).then_inc(ld_108, 16)
            act.dma_start(b2_s[:, :], b2).then_inc(ld_b2, 16)
            act.dma_start(pkl[:, :], late128).then_inc(ld_late, 16)

            def cut_high(dst, src, done):
                nc.scalar.activation(dst, src, ACT.Copy).then_inc(done, 1)

            def deviation(t):
                rows = TT[t][1]
                act.wait_ge(var_ready[0], t + 1)
                nc.scalar.activation(sd[0][:rows, t:t + 1], mv[0][:rows, t, 1:2], ACT.Sqrt,
                                     bias=eps_s[:rows, :]).then_inc(sd_ready[0], 1)

            def high_w1(q):
                act.wait_ge(ld_w1[q], 16)
                cut_high(w1_h[:, :, q * W1P:(q + 1) * W1P], piece1(q), w1_hi)

            def high_w2(q):
                act.wait_ge(ld_w2[q], 16)
                cut_high(w2_hl[:, q * W2P:(q + 1) * W2P, 0, :], piece2(q), w2_hi)

            def cut_tile(n, t, done, b):
                s, rows = TT[t]
                act.wait_ge(done, t + 1)
                nc.scalar.activation(xth[:, :, s:s + rows], transposed(b, rows), ACT.Copy).then_inc(hi_ready[n], 1)

            def keep(t, b):
                s, rows = TT[t]
                nc.scalar.activation(xt32[:, :, s:s + rows], transposed(b, rows), ACT.Copy).then_inc(xt_ready, 1)

            tables = [ACT.Sqrt, ACT.Silu, ACT.Exp, ACT.Gelu]

            def load_table(function):
                nc.scalar.activation(scrap[:, tables.index(function)][:, None], eps_s[:, :], function)

            def filter_spectrum():
                act.wait_ge(spec_mm, 1)
                nc.scalar.activation(spec_s[:, :, :], bank[5][:PF, :2 * D].rearrange("p (a d) -> p a d", a=2),
                                     ACT.Copy).then_inc(spec_ev, 1)

            def exponentials(c):
                ts = CHUNKS[c]
                w = slice(ts[0], ts[-1] + 1)
                act.wait_ge(dl_ready, c + 1)
                nc.scalar.activation(ex[:, w, :], dl[:, w, :], ACT.Exp).then_inc(exp_done, 1)

            act.wait_ge(eps_set, 1)
            load_table(ACT.Sqrt)
            deviation(0)
            act.wait_ge(ld_win, 16)
            cut_high(win_h[:, 0, :], win_s[:, 0, :], win_hi)
            deviation(1)
            cut_high(win_h[:, 1, :], win_s[:, 1, :], win_hi)
            cut_tile(0, 0, tr_done, 2)
            keep(0, 2)
            deviation(2)
            filter_spectrum()
            cut_tile(0, 1, tr_done, 3)
            keep(1, 3)
            act.wait_ge(ld_128, 16)
            act.wait_ge(ld_b2, 16)
            cut_high(rw_hl[:, :, 0, :], rw_s, sm_hi)
            cut_high(b2_hl[:, 0, :], b2_s[:, :], sm_hi)
            high_w1(0)
            cut_tile(0, 2, tr_done, 2)
            keep(2, 2)
            deviation(3)
            high_w1(1)
            load_table(ACT.Silu)

            def taps(h):
                act.wait_ge(xt_ready, (3, NT)[h])
                if h == 0:
                    act.wait_ge(tok_done, NT)
                else:
                    act.wait_ge(xs_step, 4)
                c = slice(h * HALF, (h + 1) * HALF)
                for k, (xs, x, w, bias, rows) in enumerate(((xs_a, xt32[:, 0], P_WSA, P_BSA, DA),
                                                            (xs_b, xt32[:DB, 1], P_WSB, P_BSB, DB))):
                    nc.scalar.activation(xs[:, c], x[:, c], ACT.Identity, bias=par_s[:rows, bias:bias + 1],
                                         scale=par_s[:rows, w + 1:w + 2])
                    nc.scalar.activation(outer[k][0], x[:, c], ACT.Copy, scale=par_s[:rows, w:w + 1])
                    nc.scalar.activation(outer[k][1], x[:, c], ACT.Copy, scale=par_s[:rows, w + 2:w + 3]).then_inc(xs_mid, 1)

            def project(p):
                act.wait_ge(px_done, p + 1)
                nc.scalar.activation(xp_s[:PTOK, 2 * p:2 * p + 2, :], bank[4][:PTOK, :2 * D].rearrange("p (a d) -> p a d", a=2),
                                     ACT.Copy).then_inc(px_ev, 1)

            def silu_a(h):
                act.wait_ge(gate_mm, 5 * h + 1)
                nc.scalar.activation(zs_a[:, h, :], bank[6 + (5 * h) % 2][:, :HALF], ACT.Silu,
                                     bias=par_s[:, P_BZA:P_BZA + 1]).then_inc(silu_done, 1)

            def silu_b(h):
                act.wait_ge(gate_mm, 5 * h + 2)
                nc.scalar.activation(zs_b[64:128, h, :], bank[6 + (5 * h + 1) % 2][0:64, :HALF], ACT.Silu,
                                     bias=par_s[0:64, P_BZB:P_BZB + 1]).then_inc(silu_done, 1)

            project(0)
            cut_tile(0, 3, tr_done, 3)
            keep(3, 3)
            silu_a(0)
            silu_b(0)
            project(1)
            cut_tile(0, 4, tr_done, 2)
            keep(4, 2)
            high_w1(2)
            taps(0)
            high_w1(3)
            project(2)
            silu_a(1)
            high_w1(4)
            silu_b(1)
            project(3)
            high_w1(5)
            taps(1)
            cut_tile(1, 0, tr2_done, TR2_BANK[0])
            cut_tile(1, 1, tr2_done, TR2_BANK[1])
            load_table(ACT.Exp)
            high_w2(0)
            exponentials(0)
            load_table(ACT.Gelu)

            def gelu(i):
                c, j = steps[i]
                w = chunk_cols(c)[1]
                act.wait_ge(up_done, i + 1)
                if i >= GE_RING:
                    act.wait_ge(gm_done, i - GE_RING + 1)
                nc.scalar.activation(ge[:, i % GE_RING, :w], bank[6 + i % 2][:, :w], ACT.Gelu,
                                     bias=par_s[:, P_B1 + j:P_B1 + j + 1]).then_inc(gelu_done, 1)

            def high(i):
                w = chunk_cols(steps[i][0])[1]
                act.wait_ge(gm_done, i + 1)
                if i >= RING:
                    act.wait_ge(down_done, i - RING + 1)
                nc.scalar.activation(gmhl[:, i % RING, :w], gm[:, i % GE_RING, :w], ACT.Copy).then_inc(gmh_done, 1)

            for i in range(NS + HIGH_LAG):
                if i < NS:
                    gelu(i)
                if i >= HIGH_LAG:
                    high(i - HIGH_LAG)
                if i in W2_STEPS:
                    high_w2(W2_STEPS[i])
                if i - TR2_LAG in LN2_STEPS:
                    t = LN2_STEPS[i - TR2_LAG]
                    cut_tile(1, t, tr2_done, TR2_BANK[t])

        @block.vector
        def _(dve):
            v = nc.vector
            v.memset(idle[:, :], 0.0).then_inc(idle_set, 1)

            def stats(n, tiles, src):
                for t in tiles:
                    rows = TT[t][1]
                    dve.wait_ge((h_ready, h2_ready)[n], t + 1)
                    v.bn_stats(st[n][:rows, t, :], src[:rows, t, :]).then_inc(stat[n], 1)
                for t in tiles:
                    rows = TT[t][1]
                    dve.wait_ge(stat[n], t + 1)
                    v.bn_aggr(mv[n][:rows, t, :], st[n][:rows, t, :]).then_inc(var_ready[n], 1)

            def embed(t):
                rows = TT[t][1]
                dve.wait_ge(tok_done, t + 1)
                v.tensor_tensor(h_s[:rows, t, :], bank[t % 2][:rows, :D], tokb_s[:rows, :], ALU.add).then_inc(h_ready, 1)
                stats(0, (t,), h_s)

            def normalise(n, t, src):
                rows = TT[t][1]
                if n == 0 and t < NT - 1:
                    dve.wait_ge(sd_ready[0], t + 1)
                    v.reciprocal(rs[n][:rows, t:t + 1], sd[n][:rows, t:t + 1]).then_inc(rs_ready[n], 1)
                dve.wait_ge(rs_ready[n], t + 1)
                v.tensor_scalar(xn[:rows, t, :DA], src[:rows, t, :DA], mv[n][:rows, t, 0:1], rs[n][:rows, t:t + 1],
                                ALU.subtract, ALU.mult).then_inc(xn_ready[n], 1)
                v.tensor_scalar(xn[:rows, t, DA:].rearrange("p (a d) -> p a d", a=2),
                                src[:rows, t:t + 1, DA:].broadcast_to([rows, 2, DB]), mv[n][:rows, t, 0:1],
                                rs[n][:rows, t:t + 1], ALU.subtract, ALU.mult).then_inc(xn_ready[n], 1)

            def cut(n, t):
                s, rows = TT[t]
                c = slice(s, s + rows)
                dve.wait_ge(hi_ready[n], t + 1)
                if n == 0:
                    dve.wait_ge(xt_ready, t + 1)
                    src = xt32[:, :, c]
                else:
                    src = transposed(TR2_BANK[t], rows)
                v.tensor_tensor(xtl[:, c], src[:, 0], xth[:, 0, c].bitcast(f32), ALU.subtract).then_inc(split[n], 1)
                v.tensor_tensor(xth[64:128, 1, c], src[64:128, 1], xth[64:128, 1, c].bitcast(f32),
                                ALU.subtract).then_inc(split[n], 1)

            def spectrum(p, parts=(0, 1)):
                dve.wait_ge(fwd_done, p + 1)
                dve.wait_ge(spec_ev, 1)
                for k in parts:
                    v.tensor_tensor(p_s[k][:, 2 * p:2 * p + 2, :], bank[5][:PF, :2 * D].rearrange("p (a d) -> p a d", a=2),
                                    spec_s[:, k:k + 1, :].broadcast_to([PF, 2, D]), ALU.mult).then_inc(spec_mul, 1)

            def gate_bank(h, m):
                return bank[6 + (5 * h + m) % 2]

            def first_gate_b(h):
                dve.wait_ge(silu_done, 2 * h + 2)
                v.scalar_tensor_tensor(u_b[:, h, :], gate_bank(h, 1)[64:128, :HALF], par_s[64:128, P_BZB:P_BZB + 1],
                                       zs_b[64:128, h, :], ALU.add, ALU.mult).then_inc(gate_done, 1)

            def first_gate_a(h):
                dve.wait_ge(gate_mm, 5 * h + 3)
                v.scalar_tensor_tensor(u_a[:, h, :], gate_bank(h, 2)[:, :HALF], par_s[:, P_BV1A:P_BV1A + 1],
                                       zs_a[:, h, :], ALU.add, ALU.mult).then_inc(gate_done, 1)

            def second_gate_a(h):
                dve.wait_ge(gate_mm, 5 * h + 4)
                dve.wait_ge(gate_done, 4 * h + 2)
                v.scalar_tensor_tensor(g_a[:, h, :], gate_bank(h, 3)[:, :HALF], par_s[:, P_BV2A:P_BV2A + 1],
                                       u_a[:, h, :], ALU.add, ALU.mult).then_inc(gate_done, 1)

            def second_gate_b(h):
                dve.wait_ge(gate_mm, 5 * h + 5)
                v.scalar_tensor_tensor(g_b[:, h, :], gate_bank(h, 4)[0:DB, :HALF], par_s[0:DB, P_BV2B:P_BV2B + 1],
                                       u_b[:, h, :], ALU.add, ALU.mult).then_inc(gate_done, 1)

            def mix(h, k):
                c = slice(h * HALF, (h + 1) * HALF)
                y, g, r = ((y_a, g_a, DA), (y_b, g_b, DB))[k]
                dve.wait_ge(inv_done[k], h + 1)
                dve.wait_ge(gate_done, 4 * h + 3 + k)
                v.tensor_tensor(y[:, c], bank[k][:r, :HALF], g[:, h, :], ALU.mult).then_inc(y_done[k], 1)

            def add_short(h, k):
                c = slice(h * HALF, (h + 1) * HALF)
                yt, y, xs = ((yt_a, y_a, xs_a), (yt_b, y_b, xs_b))[k]
                dve.wait_ge(y_done[k], h + 1)
                dve.wait_ge(xs_step, 4 * h + 3 + k)
                v.tensor_tensor(yt[:, c], y[:, c], xs[:, c], ALU.add).then_inc(yt_done, 1)

            def residual(t):
                rows = TT[t][1]
                dve.wait_ge(wo_done, t + 1)
                dve.wait_ge(hb_ready, t + 1)
                v.tensor_tensor(h2_s[:rows, t, :], bank[MERGE_BANK[t]][:rows, :D], hb_s[:rows, t, :],
                                ALU.add).then_inc(h2_ready, 1)

            def logits(c):
                ts = CHUNKS[c]
                n, w = len(ts), slice(ts[0], ts[-1] + 1)
                dve.wait_ge(lg_set, 1)
                dve.wait_ge(rt_done, c + 1)
                groups = ((128, ts),) if c == 0 else ((128, ts[:-1]), (TT[-1][1], ts[-1:]))
                for part in range(2):
                    for k, (rows, tiles) in enumerate(groups):
                        g, m = slice(tiles[0], tiles[-1] + 1), len(tiles)
                        src = bank[5][:rows, :2 * E * NT].rearrange("p (t a e) -> p t a e", a=2, e=E)[:, g, part]
                        other = lg[:rows, g, :] if part else rb_s[:rows, None, :].broadcast_to([rows, m, E])
                        if part:
                            dve.wait_ge(lg_ev[c], k + 1)
                        v.tensor_tensor(lg[:rows, g, :], src, other, ALU.add).then_inc(lg_ev[c], 1)
                dve.wait_ge(lg_ev[c], 2 * len(groups))
                for t in ts:
                    v.max(mx[:, t, :], lg[:, t, :]).then_inc(mx_ready, 1)
                dve.wait_ge(mx_ready, ts[-1] + 1)
                v.tensor_tensor(dl[:, w, :], lg[:, w, :], mx[:, w, 0:1].broadcast_to([128, n, E]), ALU.subtract).then_inc(dl_ready, 1)
                for t in ts:
                    last = v.max_index(ix[:, t, :], mx[:, t, :], lg[:, t, :])
                last.then_inc(ix_ready, 1)
                dve.wait_ge(ix_ready, 2 * c + 1)
                v.tensor_copy(ixf[:, w, :], ix[:, w, 0:2]).then_inc(ix_ready, 1)
                dve.wait_ge(ix_ready, 2 * c + 2)
                iota = iota_s[:, None, :].broadcast_to([128, n, E])
                v.tensor_tensor(m1[:, w, :], iota, ixf[:, w, 0:1].broadcast_to([128, n, E]), ALU.is_equal).then_inc(best, 1)
                v.tensor_tensor(m2[:, w, :], iota, ixf[:, w, 1:2].broadcast_to([128, n, E]), ALU.is_equal).then_inc(best, 1)
                dve.wait_ge(best, 4 * c + 2)
                v.tensor_tensor(mk[:, w, :], m1[:, w, :], m2[:, w, :], ALU.add).then_inc(best, 1)

            def gate_values(c):
                ts = CHUNKS[c]
                n, w = len(ts), slice(ts[0], ts[-1] + 1)
                dve.wait_ge(exp_done, c + 1)
                v.reduce_sum(se[:, w], ex[:, w, :], axis=AX.X).then_inc(sum_ready, 1)
                dve.wait_ge(best, 4 * c + 3)
                v.tensor_tensor(em[:, w, :], ex[:, w, :], mk[:, w, :], ALU.mult).then_inc(best, 1)
                dve.wait_ge(sum_ready, 2 * c + 1)
                v.reciprocal(re[:, w], se[:, w]).then_inc(sum_ready, 1)
                dve.wait_ge(best, 4 * c + 4)
                dve.wait_ge(sum_ready, 2 * c + 2)
                v.tensor_tensor(gt[:, w, :], em[:, w, :], re[:, w, None].broadcast_to([128, n, E]), ALU.mult).then_inc(ghl_ready, 1)
                dve.wait_ge(ghl_ready, 3 * c + 1)
                v.tensor_copy(ghl[:, w, 0:E].bitcast(f32r), gt[:, w, :]).then_inc(ghl_ready, 1)
                dve.wait_ge(ghl_ready, 3 * c + 2)
                v.tensor_tensor(ghl[:, w, E:2 * E], gt[:, w, :], ghl[:, w, 0:E], ALU.subtract).then_inc(ghl_ready, 1)

            def gates_down(c):
                s, cols = chunk_cols(c)
                dve.wait_ge(gtr_done, c + 1)
                v.tensor_copy(gT[:, s:s + cols], bank[5][:2 * E, :cols]).then_inc(gT_ready, 1)

            def weigh(i):
                w = chunk_cols(steps[i][0])[1]
                dve.wait_ge(gelu_done, i + 1)
                dve.wait_ge(gb_done, spread_of(i) + 1)
                v.tensor_tensor(gm[:, i % GE_RING, :w], bank[(spread_of(i) + 1) % 2][:, :w], ge[:, i % GE_RING, :w],
                                ALU.mult).then_inc(gm_done, 1)

            def low(i):
                c = steps[i][0]
                ts = CHUNKS[c]
                dve.wait_ge(gmh_done, i + 1)
                for run in ((ts[:-1], ts[-1:]) if stacks(ts[-1]) else (ts,)):
                    src = slice(high_cols(c, run[0]).start, high_cols(c, run[-1]).stop)
                    dst = slice(low_cols(c, run[0]).start, low_cols(c, run[-1]).stop)
                    last = v.tensor_tensor(gmhl[:, i % RING, dst], gm[:, i % GE_RING, src],
                                           gmhl[:, i % RING, src].bitcast(f32), ALU.subtract)
                last.then_inc(gml_done, 1)

            def fold(c, k):
                t = CHUNKS[c][k]
                rows = TT[t][1]
                dve.wait_ge(down_done, c * HC + FOLD[c][k])
                b = bank[ACC_BANK[0][t]]
                for part in (1, 0):
                    if stacks(t):
                        src = b[part * rows:(part + 1) * rows, :D]
                    else:
                        src = b[:rows, part * D:(part + 1) * D]
                    v.tensor_tensor(h2_s[:rows, t, :], src, h2_s[:rows, t, :], ALU.add).then_inc(folded, 1)
                    dve.wait_ge(folded, 2 * t + 2 - part)

            def finish(c):
                for k, t in enumerate(CHUNKS[c]):
                    rows = TT[t][1]
                    if k < len(CHUNKS[c]) - 1:
                        dve.wait_ge(acc_done, t + 1 - c)
                    else:
                        dve.wait_ge(down_done, (c + 1) * HC)
                    v.tensor_tensor(o_s[:rows, t, :], bank[ACC_BANK[1][t]][:rows, :D], h2_s[:rows, t, :],
                                    ALU.add).then_inc(fin_done, 1)

            dve.wait_ge(ld_128, 16)
            embed(0)
            normalise(0, 0, h_s)
            embed(1)
            normalise(0, 1, h_s)
            embed(2)
            cut(0, 0)
            normalise(0, 2, h_s)
            cut(0, 1)
            embed(3)
            cut(0, 2)
            normalise(0, 3, h_s)
            embed(4)
            normalise(0, 4, h_s)
            cut(0, 3)
            first_gate_b(0)
            spectrum(0)
            first_gate_a(0)
            second_gate_a(0)
            cut(0, 4)
            spectrum(1)
            second_gate_b(0)
            mix(0, 0)
            add_short(0, 0)
            mix(0, 1)
            add_short(0, 1)
            spectrum(2)
            first_gate_b(1)
            residual(0)
            stats(1, (0,), h2_s)
            spectrum(3, (0,))
            residual(1)
            stats(1, (1,), h2_s)
            spectrum(3, (1,))
            normalise(1, 0, h2_s)
            normalise(1, 1, h2_s)
            first_gate_a(1)
            cut(1, 0)
            cut(1, 1)
            second_gate_a(1)
            second_gate_b(1)
            logits(0)
            gate_values(0)
            mix(1, 1)
            gates_down(0)
            mix(1, 0)
            add_short(1, 1)
            add_short(1, 0)
            for i in range(NS + 1):
                if i - TR2_LAG in LN2_STEPS:
                    cut(1, LN2_STEPS[i - TR2_LAG])
                if i < NS:
                    weigh(i)
                if i == ROUTE_STEP + 7:
                    gates_down(1)
                for c in range(len(CHUNKS)):
                    for k in range(len(CHUNKS[c])):
                        if i == c * HC + FOLD[c][k] + DOWN_LAG - 2:
                            fold(c, k)
                if i == HC + DOWN_LAG - 2:
                    finish(0)
                if i >= 1:
                    low(i - 1)
                if i == 1:
                    residual(2)
                    residual(3)
                    residual(4)
                if i in LN2_STEPS:
                    stats(1, (LN2_STEPS[i],), h2_s)
                if i - 1 in LN2_STEPS:
                    normalise(1, LN2_STEPS[i - 1], h2_s)
                if i == ROUTE_STEP:
                    logits(1)
                if i == ROUTE_STEP + 5:
                    gate_values(1)
            finish(1)

        @block.tensor
        def _(pe):
            mm = nc.tensor.matmul

            def five(dst, rows, cols, n, w_h, w_l, x_side, start=True, stop=True):
                terms = ((xth[:, 0], w_h[:, 0]), (xth[:, 0], w_l[:, 0]), (xtl, w_h[:, 0]),
                         (xth[:, 1], w_h[:, 1]), (xth[:, 1], w_l[:, 1]))
                for k, (x, w) in enumerate(terms):
                    a, b = x[:, rows], w[:, cols]
                    if x_side == "moving":
                        a, b = b, a
                    last = mm(dst, a, b, start=start and k == 0, stop=stop and k == len(terms) - 1)
                return last

            pe.wait_ge(idle_set, 1)
            for _ in range(WARM):
                mm(bank[7][:, :], idle[:, :128], idle[:, :], start=True, stop=True)

            def filter_spectrum():
                pe.wait_ge(ld_65, 16)
                for k in range(2):
                    last = mm(bank[5][:PF, k * D:(k + 1) * D], basis_s[:, k, :], waug_s, start=True, stop=True)
                last.then_inc(spec_mm, 1)

            def embed(t):
                s, n = TT[t]
                pe.wait_ge(ld_x[t], 16)
                if t == 0:
                    pe.wait_ge(ld_tokw, 16)
                if t >= 2:
                    pe.wait_ge(h_ready, t - 1)
                for k in range(KP):
                    if t == 0 and k == KP // 2:
                        pe.wait_ge(ld_x0_rest, 16)
                        pe.wait_ge(ld_tokw_rest, 16)
                    last = mm(bank[t % 2][:n, :D], x_s[:, KP * s + k * n:KP * s + (k + 1) * n], tokw_s[:, k, :],
                              start=k == 0, stop=k == KP - 1)
                last.then_inc(tok_done, 1)

            def transpose(n, t, b, done):
                rows = TT[t][1]
                pe.wait_ge(xn_ready[n], 2 * t + 2)
                if n == 0 and t >= 2:
                    pe.wait_ge(xt_ready, t - 1)
                if n == 1 and t == 0:
                    pe.wait_ge(px_ev, 4)
                if n == 1 and t == 1:
                    pe.wait_ge(h2_ready, 2)
                if n == 1 and t == 3:
                    pe.wait_ge(gT_ready, 1)
                if n == 1 and t >= 2:
                    pe.wait_ge(split[1], 2 * (t - 1))
                dst = transposed(b, rows)
                nc.tensor.transpose(dst[:, 0], xn[:rows, t, 0:DA], ident_s[:rows, :rows])
                nc.tensor.transpose(dst[:, 1], xn[:rows, t, DA:], ident_s[:rows, :rows]).then_inc(done, 1)

            def project(p):
                pe.wait_ge(split[0], 2 * (tile_of((2 * p + 2) * PTOK - 1) + 1))
                if p == 0:
                    pe.wait_ge(win_lo, 2)
                else:
                    pe.wait_ge(px_ev, p)
                for q in range(2):
                    g = 2 * p + q
                    last = five(bank[4][:PTOK, q * D:(q + 1) * D], slice(g * PTOK, (g + 1) * PTOK), slice(0, D), 0,
                                win_h, win_l, "stationary")
                last.then_inc(px_done, 1)

            def forward(p):
                pe.wait_ge(px_ev, p + 1)
                if p == 0:
                    pe.wait_ge(ld_binx, 16)
                    pe.wait_ge(ld_108, 16)
                    pe.wait_ge(spec_ev, 1)
                else:
                    pe.wait_ge(spec_mul, 2 * p)
                mm(bank[5][:PF, :2 * D], fwd_s, xp_s[:, 2 * p:2 * p + 2, :], start=True, stop=True).then_inc(fwd_done, 1)

            def gate(h, m):
                i = 5 * h + m
                if m == 0:
                    pe.wait_ge(split[0], 2 * (tile_of((h + 1) * HALF - 1) + 1))
                if i == 0:
                    pe.wait_ge(win_lo, 2)
                if i >= 2:
                    j = i - 2
                    if j % 5 == 0:
                        pe.wait_ge(silu_done, 2 * (j // 5) + 1)
                    else:
                        pe.wait_ge(gate_done, 4 * (j // 5) + j % 5)
                c0, w = GATE_COL[m]
                five(bank[6 + i % 2][:w, :HALF], slice(h * HALF, (h + 1) * HALF), slice(c0, c0 + w), 0,
                     win_h, win_l, "moving").then_inc(gate_mm, 1)

            def inverse(h, k, pairs=range(PAIRS // 2)):
                pe.wait_ge(spec_mul, 4 * (h + 1))
                if h == 0:
                    pe.wait_ge(h_ready, NT)
                else:
                    pe.wait_ge(y_done[k], 1)
                d0, d1 = ((0, DA), (DA, D))[k]
                for g in pairs:
                    for part in range(2):
                        last = mm(bank[k][:d1 - d0, g * PTOK:(g + 1) * PTOK], p_s[part][:, h * PAIRS // 2 + g, d0:d1],
                                  inv_s[:, part, :], start=part == 0, stop=part == 1)
                if g == PAIRS // 2 - 1:
                    last.then_inc(inv_done[k], 1)

            def merge(t):
                s, n = TT[t]
                pe.wait_ge(yt_done, 2 * ((s + n - 1) // HALF + 1))
                if t == 2:
                    pe.wait_ge(split[1], 4)
                if t < 2:
                    pe.wait_ge(xt_ready, NT)
                    pe.wait_ge(ld_late, 16)
                elif t < 4:
                    pe.wait_ge(h2_ready, t - 1)
                b = bank[MERGE_BANK[t]][:n, :D]
                mm(b, yt_a[:, s:s + n], woa_s, start=True, stop=False)
                mm(b, yt_b[:, s:s + n], wob_s, start=False, stop=True).then_inc(wo_done, 1)

            def logits(c):
                if c == 0:
                    pe.wait_ge(sm_lo, 2)
                    pe.wait_ge(spec_mul, 8)
                pe.wait_ge(split[1], 2 * (CHUNKS[c][-1] + 1))
                for t in CHUNKS[c]:
                    s, n = TT[t]
                    dst = bank[5][:n, 2 * t * E:2 * (t + 1) * E]
                    mm(dst, xth[:, 0, s:s + n], rw_hl[:, 0, :, :], start=True, stop=False)
                    mm(dst[:, :E], xtl[:, s:s + n], rw_hl[:, 0, 0, :], start=False, stop=False)
                    last = mm(dst, xth[:, 1, s:s + n], rw_hl[:, 1, :, :], start=False, stop=True)
                last.then_inc(rt_done, 1)

            def gates_across(c):
                pe.wait_ge(ghl_ready, 3 * c + 3)
                s0 = chunk_cols(c)[0]
                for t in CHUNKS[c]:
                    s, n = TT[t]
                    last = nc.tensor.transpose(bank[5][:2 * E, s - s0:s - s0 + n], ghl[:n, t, :], ident_s[:n, :n])
                last.then_inc(gtr_done, 1)

            def up(i):
                c, j = steps[i]
                s, w = chunk_cols(c)
                if i == 0:
                    pe.wait_ge(gate_done, 8)
                if i >= 2:
                    pe.wait_ge(gelu_done, i - 1)
                if c == 0 and j % 3 == 0:
                    pe.wait_ge(w1_lo, j // 3 + 1)
                five(bank[6 + i % 2][:, :w], slice(s, s + w), slice(j * 128, (j + 1) * 128), 1, w1_h, w1_l,
                     "moving").then_inc(up_done, 1)

            def spread(i):
                n = spread_of(i)
                if i > 0 and spread_of(i - 1) == n:
                    return
                c, q = spreads[n]
                s, w = chunk_cols(c)
                if n == 0:
                    pe.wait_ge(ld_sel, 16)
                if n < 2:
                    pe.wait_ge(y_done[(n + 1) % 2], 2)
                else:
                    c0, q0 = spreads[n - 2]
                    pe.wait_ge(gm_done, c0 * HC + SPREAD_TILES[q0][-1] + 1)
                if q == 0:
                    pe.wait_ge(gT_ready, c + 1)
                mm(bank[(n + 1) % 2][:, :w], sel_r[:, q * 128:(q + 1) * 128], gT[:, s:s + w], start=True,
                   stop=True).then_inc(gb_done, 1)

            def down(i):
                c, j = steps[i]
                pe.wait_ge(gmh_done, i + 1)
                pe.wait_ge(gml_done, i + 1)
                if c == 0 and j % 3 == 0:
                    pe.wait_ge(w2_lo, j // 3 + 1)
                r = i % RING
                for k, t in enumerate(CHUNKS[c]):
                    s, n = TT[t]
                    if j == 0 and t < 2:
                        pe.wait_ge(h2_ready, NT)
                    elif j == 0 and t == 2:
                        pe.wait_ge(folded, 4)
                    elif j == 0 and t == 3:
                        pe.wait_ge(gT_ready, 2)
                    elif j == 0 and t == 4:
                        pe.wait_ge(fin_done, 1)
                    if j == FOLD[c][k] and t == 0:
                        pe.wait_ge(split[1], 2 * NT)
                    elif j == FOLD[c][k] and t == 2:
                        pe.wait_ge(fin_done, 2)
                    elif j == FOLD[c][k]:
                        pe.wait_ge(folded, 2 * t)
                    b = bank[ACC_BANK[j >= FOLD[c][k]][t]]
                    acc, both = b[:n, :D], b[:n, :2 * D]
                    high, low = (gmhl[:, r, cols(c, t)] for cols in (high_cols, low_cols))
                    if j == 0 and stacks(t):
                        pe.wait_ge(no_gates_set, 1)
                        mm(b[:2 * n, :D], gT[:, s:s + 2 * n], b2_hl[:, 0, :], start=True, stop=False)
                        mm(acc, gT[:, s:s + n], b2_hl[:, 1, :], start=False, stop=False)
                    elif j == 0:
                        mm(both, gT[:, s:s + n], b2_hl[:, :, :], start=True, stop=False)
                    if j < FOLD[c][k] and stacks(t):
                        mm(acc, high, w2_hl[:, j, 1, :], start=False, stop=False)
                        last = mm(b[:2 * n, :D], gmhl[:, r, high_cols(c, t).start:low_cols(c, t).stop], w2_hl[:, j, 0, :],
                                  start=False, stop=j == FOLD[c][k] - 1)
                        continue
                    if j < FOLD[c][k]:
                        mm(both, high, w2_hl[:, j, :, :], start=False, stop=False)
                    else:
                        mm(acc, high, w2_hl[:, j, 0, :], start=j == FOLD[c][k], stop=False)
                        mm(acc, high, w2_hl[:, j, 1, :], start=False, stop=False)
                    last = mm(acc, low, w2_hl[:, j, 0, :], start=False, stop=j in (FOLD[c][k] - 1, HC - 1))
                    if j == HC - 1 and k < len(CHUNKS[c]) - 1:
                        last.then_inc(acc_done, 1)
                last.then_inc(down_done, 1)

            embed(0)
            embed(1)
            embed(2)
            pe.wait_ge(ld_128, 16)
            transpose(0, 0, 2, tr_done)
            filter_spectrum()
            transpose(0, 1, 3, tr_done)
            embed(3)
            transpose(0, 2, 2, tr_done)
            embed(4)
            project(0)
            gate(0, 0)
            transpose(0, 3, 3, tr_done)
            gate(0, 1)
            project(1)
            transpose(0, 4, 2, tr_done)
            forward(0)
            gate(0, 2)
            gate(0, 3)
            forward(1)
            gate(0, 4)
            project(2)
            gate(1, 0)
            inverse(0, 0)
            inverse(0, 1)
            forward(2)
            gate(1, 1)
            project(3)
            merge(0)
            forward(3)
            merge(1)
            gate(1, 2)
            gate(1, 3)
            inverse(1, 1, range(0, 2))
            transpose(1, 0, TR2_BANK[0], tr2_done)
            inverse(1, 1, range(2, 3))
            transpose(1, 1, TR2_BANK[1], tr2_done)
            inverse(1, 1, range(3, 4))
            gate(1, 4)
            inverse(1, 0, range(0, 1))
            logits(0)
            inverse(1, 0, range(1, PAIRS // 2))
            for i in range(NS + DOWN_LAG):
                if i < NS:
                    up(i)
                if i == 1:
                    gates_across(0)
                if i == 2:
                    spread(0)
                if 3 <= i < NS - 1:
                    spread(i - 1)
                if i == 3:
                    merge(2)
                    merge(3)
                    merge(4)
                if i >= DOWN_LAG:
                    down(i - DOWN_LAG)
                if i in (NS - 1, NS):
                    spread(i - 1)
                if i - TR2_LAG in LN2_STEPS:
                    t = LN2_STEPS[i - TR2_LAG]
                    transpose(1, t, TR2_BANK[t], tr2_done)
                if i == ROUTE_STEP + 2:
                    logits(1)
                if i == ROUTE_STEP + 8:
                    gates_across(1)


def hidden_order():
    import numpy as np
    units = np.arange(E * HID).reshape(E, HID)
    whole = HID // 128 * 128
    return np.concatenate([units[:, :whole].reshape(-1), units[:, whole:].reshape(-1)])


def constants():
    import numpy as np
    k = np.arange(SEQ)
    f_cos, f_sin = np.arange(POINTS // 2 + 1), np.arange(1, POINTS // 2)
    turn = 2 * np.pi / POINTS
    trig = np.concatenate([np.cos(turn * np.outer(f_cos, k)), np.sin(turn * np.outer(f_sin, k))])
    pos = np.sin(np.outer(k, np.arange(TAPS)) / TAPS)
    pos = np.concatenate([pos, np.ones((SEQ, 1))], 1)
    f_all = np.concatenate([f_cos, f_sin])
    basis = np.stack([np.cos(turn * np.outer(f_all, k)) @ pos, np.sin(turn * np.outer(f_all, k)) @ pos])
    basis = np.concatenate([basis, basis], 1).transpose(2, 0, 1)
    fwd = np.zeros((PTOK + 1, PF))
    inv = np.zeros((PF, 2, PTOK))
    theta = turn * np.outer(f_all, k - SEQ // 2)
    weight = np.where((f_all == 0) | (f_all == POINTS // 2), 1.0, 2.0)[:, None] / POINTS
    is_cos = (np.arange(POINTS) < len(f_cos))[:, None]
    first = weight * np.where(is_cos, np.cos(theta), np.sin(theta))
    second = weight * np.where(is_cos, -np.sin(theta), np.cos(theta))
    for b in range(2):
        rows, cols = slice(b * SEQ, (b + 1) * SEQ), slice(b * POINTS, (b + 1) * POINTS)
        fwd[rows, cols] = trig.T
        inv[cols, 0, rows] = first
        inv[cols, 1, rows] = second
    fwd[PTOK] = fwd.sum(0)
    expert = hidden_order() // HID
    expert = np.concatenate([expert[tiles[0] * 128:(tiles[0] + 1) * 128] for tiles in SPREAD_TILES])
    sel = np.tile((np.arange(E)[:, None] == expert[None, :]), (2, 1))
    made = dict(basis=basis.reshape(TAPS + 1, -1), fwd=fwd, inv=inv.reshape(PF, -1), ident=np.eye(128),
                iota=np.tile(np.arange(E), (128, 1)), sel=sel)
    return {n: np.ascontiguousarray(a, dtype=np.float32) for n, a in made.items()}


def kernel(x, L0_tok_W, L0_tok_b, L0_attn_w_in, L0_attn_b_in, L0_attn_w_filt, L0_attn_b_filt,
           L0_attn_w_short, L0_attn_b_short, L0_attn_w_out, L0_attn_b_out, L0_ffn_router_w,
           L0_ffn_router_b, L0_ffn_w1, L0_ffn_b1, L0_ffn_w2, L0_ffn_b2):
    import numpy as np
    import concourse.bacc as bacc
    from concourse.bass_utils import run_bass_kernel_spmd

    def split_rows(w, twice):
        return w[:DA], np.concatenate([w[DA:], w[DA:]]) if twice else w[DA:]

    a = {k: np.asarray(v) for k, v in locals().items() if k == "x" or k.startswith("L0_")}
    patches = a["x"].reshape(IMAGES, 3, 6, 16, 6, 16).transpose(1, 3, 5, 0, 2, 4).reshape(KP, 128, TOK)
    xt = np.concatenate([patches[:, :, s:s + n].transpose(1, 0, 2).reshape(128, KP * n) for s, n in TT], 1)
    order = np.concatenate([np.arange(0, D), D + np.arange(DA), D + np.arange(DA, D), 2 * D + np.arange(DA, D),
                            2 * D + np.arange(DA), 3 * D + np.arange(DA), 3 * D + np.arange(DA, D)])
    win_a, win_b = split_rows(a["L0_attn_w_in"][:, order], True)
    b_in, w_short, b_short = a["L0_attn_b_in"], a["L0_attn_w_short"][:, 0, :], a["L0_attn_b_short"]
    par = np.zeros((128, NPAR), np.float32)
    par[:, P_BZA] = b_in[D:D + DA]
    par[:, P_BZB] = np.concatenate([b_in[D + DA:2 * D], b_in[2 * D + DA:3 * D]])
    par[:, P_BV1A] = b_in[2 * D:2 * D + DA]
    par[:, P_BV2A] = b_in[3 * D:3 * D + DA]
    par[:DB, P_BV2B] = b_in[3 * D + DA:]
    par[:, P_WSA:P_WSA + 3] = w_short[:DA]
    par[:DB, P_WSB:P_WSB + 3] = w_short[DA:]
    par[:, P_BSA] = b_short[:DA]
    par[:DB, P_BSB] = b_short[DA:]
    hidden = hidden_order()
    par[:, P_B1:] = a["L0_ffn_b1"].reshape(-1)[hidden].reshape(HC, 128).T
    wo_a, wo_b = split_rows(a["L0_attn_w_out"], False)
    rw_a, rw_b = split_rows(a["L0_ffn_router_w"], True)
    w1 = np.stack(split_rows(a["L0_ffn_w1"].transpose(1, 0, 2).reshape(D, HC * 128)[:, hidden], True), 1)
    w1 = w1.reshape(128, 2, PIECES, W1P).transpose(0, 2, 1, 3).reshape(128, PIECES, 2 * W1P)
    const = constants()

    def pack(rows, layout, **parts):
        assert {n: p.shape[1] for n, p in parts.items()} == layout, (rows, layout)
        return np.concatenate([np.pad(p, ((0, rows - len(p)), (0, 0))) for p in parts.values()], 1)

    def all_rows(row):
        return np.tile(row, (128, 1))

    arrays = dict(
        xt=xt, tokw=a["L0_tok_W"].T.reshape(KP, 128, D).transpose(1, 0, 2), win=np.stack([win_a, win_b], 1), binx=b_in[:D],
        rows128=pack(128, ROWS128, ident=const["ident"], tokb=all_rows(a["L0_tok_b"]), par=par, iota=const["iota"],
                     rb=all_rows(a["L0_ffn_router_b"]), rw=np.concatenate([rw_a, rw_b], 1)),
        rows65=pack(TAPS + 1, ROWS65, waug=np.concatenate([a["L0_attn_w_filt"], a["L0_attn_b_filt"][None]]),
                    basis=const["basis"]),
        rows108=pack(PF, ROWS108, fwd=const["fwd"], inv=const["inv"]),
        late128=pack(128, LATE128, wo_a=wo_a, wo_b=wo_b, bout=all_rows(a["L0_attn_b_out"])),
        b2=np.concatenate([a["L0_ffn_b2"]] * 2), w1=w1,
        w2=a["L0_ffn_w2"].reshape(HC * 128, D)[hidden].reshape(HC, 128, D).transpose(1, 0, 2).reshape(128, PIECES, W2P * D),
        c_sel=const["sel"])
    arrays = {k: np.ascontiguousarray(v) for k, v in arrays.items()}
    nc = bacc.Bacc("TRN2", target_bir_lowering=False, num_devices=1)
    args = [nc.dram_tensor(k, v.shape, mybir.dt.from_np(v.dtype), kind="ExternalInput").ap() for k, v in arrays.items()]
    out = nc.dram_tensor("out", (TOK, D), mybir.dt.float32, kind="ExternalOutput").ap()
    build(nc, *args, out)
    r = run_bass_kernel_spmd(nc, [arrays], core_ids=[0])
    return r.results[0]["out"].reshape(IMAGES, SEQ, D)
```
